# Optimizing a Trainium2 kernel written in Bass

```python
import numpy as np
import jax
import jax.numpy as jnp

def _softmax(x, axis=-1):
    return jax.nn.softmax(x, axis=axis)

def _gelu(x):
    return jax.nn.gelu(x, approximate=True)

def _silu(x):
    return jax.nn.silu(x)

def _sigmoid(x):
    return jax.nn.sigmoid(x)

def _layernorm(x, axis=-1, eps=1e-05):
    m = jnp.mean(x, axis=axis, keepdims=True)
    v = jnp.var(x, axis=axis, keepdims=True)
    return (x - m) / jnp.sqrt(v + eps)

def _scatter_add(tgt, idx, src, axis=0):
    return tgt.at[idx].add(src)

def _segment_sum(src, seg, n):
    return jax.ops.segment_sum(src, seg, n)
kernel_name = 'mk_dlrm_tower_d1_rec_r8_158832'

def setup_inputs(seed: int=0):
    np.random.seed(seed)
    _w = jnp.asarray

    def _rec_inputs():
        import jax
        import jax.numpy as jnp
        _tk = jax.random.key(seed)
        dense_ctx = jax.random.normal(jax.random.fold_in(_tk, 190), (2048, 16), jnp.float32)
        ids = jnp.stack([jax.random.randint(jax.random.fold_in(_tk, 200 + f), (2048,), 0, v, jnp.int32) for f, v in enumerate([125000, 1000, 12500, 1000, 125000, 1250, 125000, 1250, 1000, 1000, 1000, 1000, 1000, 1000, 1000, 1250, 1250, 12500, 1000, 1000, 1250, 1000, 1000, 1250, 12500, 12500, 12500, 1250, 1000, 1000, 12500, 1250, 12500, 1250, 1250, 1250, 1250, 1250, 1250, 1250])], axis=1)
        tbl_0 = 0.05 * jax.random.normal(jax.random.fold_in(_tk, 500 + 0), (125000, 64), jnp.float32)
        tbl_1 = 0.05 * jax.random.normal(jax.random.fold_in(_tk, 500 + 1), (1000, 64), jnp.float32)
        tbl_2 = 0.05 * jax.random.normal(jax.random.fold_in(_tk, 500 + 2), (12500, 64), jnp.float32)
        tbl_3 = 0.05 * jax.random.normal(jax.random.fold_in(_tk, 500 + 3), (1000, 64), jnp.float32)
        tbl_4 = 0.05 * jax.random.normal(jax.random.fold_in(_tk, 500 + 4), (125000, 64), jnp.float32)
        tbl_5 = 0.05 * jax.random.normal(jax.random.fold_in(_tk, 500 + 5), (1250, 64), jnp.float32)
        tbl_6 = 0.05 * jax.random.normal(jax.random.fold_in(_tk, 500 + 6), (125000, 64), jnp.float32)
        tbl_7 = 0.05 * jax.random.normal(jax.random.fold_in(_tk, 500 + 7), (1250, 64), jnp.float32)
        tbl_8 = 0.05 * jax.random.normal(jax.random.fold_in(_tk, 500 + 8), (1000, 64), jnp.float32)
        tbl_9 = 0.05 * jax.random.normal(jax.random.fold_in(_tk, 500 + 9), (1000, 64), jnp.float32)
        tbl_10 = 0.05 * jax.random.normal(jax.random.fold_in(_tk, 500 + 10), (1000, 64), jnp.float32)
        tbl_11 = 0.05 * jax.random.normal(jax.random.fold_in(_tk, 500 + 11), (1000, 64), jnp.float32)
        tbl_12 = 0.05 * jax.random.normal(jax.random.fold_in(_tk, 500 + 12), (1000, 64), jnp.float32)
        tbl_13 = 0.05 * jax.random.normal(jax.random.fold_in(_tk, 500 + 13), (1000, 64), jnp.float32)
        tbl_14 = 0.05 * jax.random.normal(jax.random.fold_in(_tk, 500 + 14), (1000, 64), jnp.float32)
        tbl_15 = 0.05 * jax.random.normal(jax.random.fold_in(_tk, 500 + 15), (1250, 64), jnp.float32)
        tbl_16 = 0.05 * jax.random.normal(jax.random.fold_in(_tk, 500 + 16), (1250, 64), jnp.float32)
        tbl_17 = 0.05 * jax.random.normal(jax.random.fold_in(_tk, 500 + 17), (12500, 64), jnp.float32)
        tbl_18 = 0.05 * jax.random.normal(jax.random.fold_in(_tk, 500 + 18), (1000, 64), jnp.float32)
        tbl_19 = 0.05 * jax.random.normal(jax.random.fold_in(_tk, 500 + 19), (1000, 64), jnp.float32)
        tbl_20 = 0.05 * jax.random.normal(jax.random.fold_in(_tk, 500 + 20), (1250, 64), jnp.float32)
        tbl_21 = 0.05 * jax.random.normal(jax.random.fold_in(_tk, 500 + 21), (1000, 64), jnp.float32)
        tbl_22 = 0.05 * jax.random.normal(jax.random.fold_in(_tk, 500 + 22), (1000, 64), jnp.float32)
        tbl_23 = 0.05 * jax.random.normal(jax.random.fold_in(_tk, 500 + 23), (1250, 64), jnp.float32)
        tbl_24 = 0.05 * jax.random.normal(jax.random.fold_in(_tk, 500 + 24), (12500, 64), jnp.float32)
        tbl_25 = 0.05 * jax.random.normal(jax.random.fold_in(_tk, 500 + 25), (12500, 64), jnp.float32)
        tbl_26 = 0.05 * jax.random.normal(jax.random.fold_in(_tk, 500 + 26), (12500, 64), jnp.float32)
        tbl_27 = 0.05 * jax.random.normal(jax.random.fold_in(_tk, 500 + 27), (1250, 64), jnp.float32)
        tbl_28 = 0.05 * jax.random.normal(jax.random.fold_in(_tk, 500 + 28), (1000, 64), jnp.float32)
        tbl_29 = 0.05 * jax.random.normal(jax.random.fold_in(_tk, 500 + 29), (1000, 64), jnp.float32)
        tbl_30 = 0.05 * jax.random.normal(jax.random.fold_in(_tk, 500 + 30), (12500, 64), jnp.float32)
        tbl_31 = 0.05 * jax.random.normal(jax.random.fold_in(_tk, 500 + 31), (1250, 64), jnp.float32)
        tbl_32 = 0.05 * jax.random.normal(jax.random.fold_in(_tk, 500 + 32), (12500, 64), jnp.float32)
        tbl_33 = 0.05 * jax.random.normal(jax.random.fold_in(_tk, 500 + 33), (1250, 64), jnp.float32)
        tbl_34 = 0.05 * jax.random.normal(jax.random.fold_in(_tk, 500 + 34), (1250, 64), jnp.float32)
        tbl_35 = 0.05 * jax.random.normal(jax.random.fold_in(_tk, 500 + 35), (1250, 64), jnp.float32)
        tbl_36 = 0.05 * jax.random.normal(jax.random.fold_in(_tk, 500 + 36), (1250, 64), jnp.float32)
        tbl_37 = 0.05 * jax.random.normal(jax.random.fold_in(_tk, 500 + 37), (1250, 64), jnp.float32)
        tbl_38 = 0.05 * jax.random.normal(jax.random.fold_in(_tk, 500 + 38), (1250, 64), jnp.float32)
        tbl_39 = 0.05 * jax.random.normal(jax.random.fold_in(_tk, 500 + 39), (1250, 64), jnp.float32)
        _rk = jax.random.fold_in(_tk, 7)
        W_top1 = 0.0354441 * jax.random.normal(jax.random.fold_in(_tk, 801), (796, 512), jnp.float32)
        W_top2 = 0.0441942 * jax.random.normal(jax.random.fold_in(_tk, 802), (512, 256), jnp.float32)
        W_top3 = 0.0625 * jax.random.normal(jax.random.fold_in(_tk, 803), (256, 1), jnp.float32)
        b_top1 = jnp.zeros((512,), jnp.float32)
        b_top2 = jnp.zeros((256,), jnp.float32)
        return (dense_ctx, ids, tbl_0, tbl_1, tbl_2, tbl_3, tbl_4, tbl_5, tbl_6, tbl_7, tbl_8, tbl_9, tbl_10, tbl_11, tbl_12, tbl_13, tbl_14, tbl_15, tbl_16, tbl_17, tbl_18, tbl_19, tbl_20, tbl_21, tbl_22, tbl_23, tbl_24, tbl_25, tbl_26, tbl_27, tbl_28, tbl_29, tbl_30, tbl_31, tbl_32, tbl_33, tbl_34, tbl_35, tbl_36, tbl_37, tbl_38, tbl_39, W_top1, b_top1, W_top2, b_top2, W_top3)
    dense_ctx, ids, tbl_0, tbl_1, tbl_2, tbl_3, tbl_4, tbl_5, tbl_6, tbl_7, tbl_8, tbl_9, tbl_10, tbl_11, tbl_12, tbl_13, tbl_14, tbl_15, tbl_16, tbl_17, tbl_18, tbl_19, tbl_20, tbl_21, tbl_22, tbl_23, tbl_24, tbl_25, tbl_26, tbl_27, tbl_28, tbl_29, tbl_30, tbl_31, tbl_32, tbl_33, tbl_34, tbl_35, tbl_36, tbl_37, tbl_38, tbl_39, W_top1, b_top1, W_top2, b_top2, W_top3 = _rec_inputs()

    def _L0_rec_setup():
        import jax, jax.numpy as jnp
        import numpy as np

        def _pair_indices(num_fields):
            i_idx, j_idx = np.triu_indices(num_fields, k=1)
            return (jnp.asarray(i_idx), jnp.asarray(j_idx))
        key = jax.random.key(seed)
        k1, k2 = jax.random.split(key)
        B, F, D = (256, 40, 64)
        P = F * (F - 1) // 2
        x = jax.random.normal(k1, (B, F, D), dtype=jnp.float32)
        W = jax.random.normal(k2, (P, D, D), dtype=jnp.float32) * (1.0 / np.sqrt(D))
        return {'x': x, 'W': W}
    _L0_rec_all = _L0_rec_setup()
    _L0_rec_in = {k: v for k, v in _L0_rec_all.items() if k in ('W',)}
    del _L0_rec_all
    return {'dense_ctx': dense_ctx, 'ids': ids, 'tbl_0': tbl_0, 'tbl_1': tbl_1, 'tbl_2': tbl_2, 'tbl_3': tbl_3, 'tbl_4': tbl_4, 'tbl_5': tbl_5, 'tbl_6': tbl_6, 'tbl_7': tbl_7, 'tbl_8': tbl_8, 'tbl_9': tbl_9, 'tbl_10': tbl_10, 'tbl_11': tbl_11, 'tbl_12': tbl_12, 'tbl_13': tbl_13, 'tbl_14': tbl_14, 'tbl_15': tbl_15, 'tbl_16': tbl_16, 'tbl_17': tbl_17, 'tbl_18': tbl_18, 'tbl_19': tbl_19, 'tbl_20': tbl_20, 'tbl_21': tbl_21, 'tbl_22': tbl_22, 'tbl_23': tbl_23, 'tbl_24': tbl_24, 'tbl_25': tbl_25, 'tbl_26': tbl_26, 'tbl_27': tbl_27, 'tbl_28': tbl_28, 'tbl_29': tbl_29, 'tbl_30': tbl_30, 'tbl_31': tbl_31, 'tbl_32': tbl_32, 'tbl_33': tbl_33, 'tbl_34': tbl_34, 'tbl_35': tbl_35, 'tbl_36': tbl_36, 'tbl_37': tbl_37, 'tbl_38': tbl_38, 'tbl_39': tbl_39, 'W_top1': W_top1, 'b_top1': b_top1, 'W_top2': W_top2, 'b_top2': b_top2, 'W_top3': W_top3, 'L0_rec_W': _L0_rec_in['W']}

def reference(dense_ctx, ids, tbl_0, tbl_1, tbl_2, tbl_3, tbl_4, tbl_5, tbl_6, tbl_7, tbl_8, tbl_9, tbl_10, tbl_11, tbl_12, tbl_13, tbl_14, tbl_15, tbl_16, tbl_17, tbl_18, tbl_19, tbl_20, tbl_21, tbl_22, tbl_23, tbl_24, tbl_25, tbl_26, tbl_27, tbl_28, tbl_29, tbl_30, tbl_31, tbl_32, tbl_33, tbl_34, tbl_35, tbl_36, tbl_37, tbl_38, tbl_39, W_top1, b_top1, W_top2, b_top2, W_top3, L0_rec_W):
    import jax
    import jax.numpy as jnp

    def _L0_rec_ref(x, W):
        import jax, jax.numpy as jnp
        import numpy as np

        def _pair_indices(num_fields):
            i_idx, j_idx = np.triu_indices(num_fields, k=1)
            return (jnp.asarray(i_idx), jnp.asarray(j_idx))
        B, F, D = x.shape
        i_idx, j_idx = _pair_indices(F)
        vi = x[:, i_idx, :]
        vj = x[:, j_idx, :]
        viW = jnp.einsum('bpd,pde->bpe', vi, W)
        out = jnp.einsum('bpe,bpe->bp', viW, vj)
        return out
    e = jnp.stack([tbl_0[ids[:, 0]], tbl_1[ids[:, 1]], tbl_2[ids[:, 2]], tbl_3[ids[:, 3]], tbl_4[ids[:, 4]], tbl_5[ids[:, 5]], tbl_6[ids[:, 6]], tbl_7[ids[:, 7]], tbl_8[ids[:, 8]], tbl_9[ids[:, 9]], tbl_10[ids[:, 10]], tbl_11[ids[:, 11]], tbl_12[ids[:, 12]], tbl_13[ids[:, 13]], tbl_14[ids[:, 14]], tbl_15[ids[:, 15]], tbl_16[ids[:, 16]], tbl_17[ids[:, 17]], tbl_18[ids[:, 18]], tbl_19[ids[:, 19]], tbl_20[ids[:, 20]], tbl_21[ids[:, 21]], tbl_22[ids[:, 22]], tbl_23[ids[:, 23]], tbl_24[ids[:, 24]], tbl_25[ids[:, 25]], tbl_26[ids[:, 26]], tbl_27[ids[:, 27]], tbl_28[ids[:, 28]], tbl_29[ids[:, 29]], tbl_30[ids[:, 30]], tbl_31[ids[:, 31]], tbl_32[ids[:, 32]], tbl_33[ids[:, 33]], tbl_34[ids[:, 34]], tbl_35[ids[:, 35]], tbl_36[ids[:, 36]], tbl_37[ids[:, 37]], tbl_38[ids[:, 38]], tbl_39[ids[:, 39]]], axis=1)
    z = _L0_rec_ref(e, L0_rec_W)
    z = z.reshape(z.shape[0], -1)
    h = jnp.concatenate([z, dense_ctx], axis=1)
    h = jnp.maximum(h @ W_top1 + b_top1, 0.0)
    h = jnp.maximum(h @ W_top2 + b_top2, 0.0)
    y = h @ W_top3
    return y

_drawn_inputs = setup_inputs


def setup_inputs(seed=0):
    import zlib

    import numpy as np

    out = dict(_drawn_inputs(seed))
    spreads = {'b_top1': (0.0, 0.1), 'b_top2': (0.0, 0.1)}
    factors = {}
    for name, (base, spread) in spreads.items():
        noise = np.random.default_rng([zlib.crc32(name.encode()), seed]).standard_normal(out[name].shape)
        drawn = base * np.exp(spread * noise) if base else spread * noise
        out[name] = jnp.asarray(drawn.astype(out[name].dtype))
    for name, factor in factors.items():
        out[name] = (out[name] * factor).astype(out[name].dtype)
    return out
```

```python
import concourse.bass as bass
from concourse import mybir
from contextlib import ExitStack

BATCH, FIELDS, DIM = 2048, 40, 64
PAIRS = FIELDS * (FIELDS - 1) // 2
DENSE, H1, H2 = 16, 512, 256
VOCAB = [125000, 1000, 12500, 1000, 125000, 1250, 125000, 1250, 1000, 1000, 1000, 1000, 1000, 1000, 1000,
         1250, 1250, 12500, 1000, 1000, 1250, 1000, 1000, 1250, 12500, 12500, 12500, 1250, 1000, 1000,
         12500, 1250, 12500, 1250, 1250, 1250, 1250, 1250, 1250, 1250]
P = 128
CB = 512
CHUNKS = BATCH // CB
SUB = CB // P
T = FIELDS // 2


def step_list():
    out = []
    for k in range(T):
        if k % 2:
            out.append(("half", k - 1, None))
        out += [("full", k, t) for t in range(k + 1, T)]
    return out


STEPS = step_list()
N = len(STEPS)
LAST_OF_K = {k: max(n for n, s in enumerate(STEPS)
                    if (s[0] == "full" and s[1] == k) or (s[0] == "half" and s[1] + 1 == k)) for k in range(T)}
FIRST_OF_K = {k: (min(n for n, s in enumerate(STEPS) if (s[0] == "full" and s[1] == k) or
                      (s[0] == "half" and s[1] + 1 == k))) for k in range(T)}

ZSTEPS = 32
ZG = -(-N // ZSTEPS)
DENSE_ROW = 96
LASTK = DENSE_ROW + DENSE


def z_place(n, h):
    g = n // ZSTEPS
    s = 2 * (n - g * ZSTEPS) + h
    ways = 3 if g == ZG - 1 else 4
    return g, s % ways, s // ways


def z_rows():
    def pair(i, j):
        return i * FIELDS - i * (i + 1) // 2 + (j - i - 1)
    out = []
    for n, (kind, k, t) in enumerate(STEPS):
        for h in (0, 1):
            g, c, q = z_place(n, h)
            row = g * P + 32 * c + 2 * q
            if kind == "full":
                out += [(row + e, pair(2 * k + h, 2 * t + e)) for e in (0, 1)]
            else:
                out.append((row + 1, pair(2 * (k + h), 2 * (k + h) + 1)))
    return out


WS = 10
WSLOTS = N // WS
WRING = 4
XRING = 4
GRING = 4
PRING = 4
UBUF = 3
TSTEPS = T // 2
TAT = [12 + 19 * i for i in range(TSTEPS)]
LAG = 2
M1, M2 = H1 // P, H2 // P
TOP_AT = 2
BATCHES = N // 2


def top_items():
    return ([(1, m, q, q == ZG - 1) for m in range(M1) for q in range(ZG)] +
            [(2, m, q, q == M1 - 1) for m in range(M2) for q in range(M1)] +
            [(3, 0, q, q == M2 - 1) for q in range(M2)])


TOPS = top_items()
TOP_GROUPS = M1 + M2 + 1


def chunk_order(top, prefetch):
    out = []
    tops = list(TOPS) if top else []
    for n in range(N):
        if n >= TOP_AT and tops:
            out.append(("top", tops.pop(0)))
        out.append(("pairs", n))
        if prefetch and n in TAT:
            out.append(("transpose", TAT.index(n)))
        if n % 2 and n >= LAG + 1:
            out.append(("sum", (n - 1 - LAG) // 2))
    out += [("sum", j) for j in range((N - LAG) // 2, BATCHES)]
    return out


def pair_tower(nc, ids, tables, w_pairs, dense, w1, b1, w2, b2, w3, y):
    f32, i32, u32 = mybir.dt.float32, mybir.dt.int32, mybir.dt.uint32
    ALU = mybir.AluOpType
    ACT = mybir.ActivationFunctionType

    ctx = ExitStack()
    with ctx:
        def sb(name, shape, dt=f32):
            return ctx.enter_context(nc.sbuf_tensor(name, shape, dt))

        def sem(name):
            return ctx.enter_context(nc.semaphore(name))

        index = sb("index", [P, CHUNKS * SUB * FIELDS], i32)
        index_now = sb("index_now", [P, SUB * FIELDS], i32)
        gathered = sb("gathered", [P, GRING, SUB, 2 * DIM])
        emb = sb("emb", [P, 2 * T, CB])
        staged = sb("staged", [P, XRING, CB])
        weights = sb("weights", [P, WRING, WS * P])
        prod = sb("prod", [P, PRING, 2, CB])
        z = sb("z", [P, ZG, CB])
        h1 = sb("h1", [P, M1, CB])
        h2 = sb("h2", [P, M2, CB])
        ysb = sb("ysb", [1, BATCH])
        w1s = sb("w1s", [P, ZG, H1])
        w2s = sb("w2s", [P, M1, H2])
        w3s = sb("w3s", [P, M2])
        b1s = sb("b1s", [P, M1])
        b2s = sb("b2s", [P, M2])
        ident = sb("ident", [P, P])
        band = sb("band", [P, 62])
        u = ctx.enter_context(nc.psum_tensor("u", [P, UBUF, 2, CB], f32))
        zacc = ctx.enter_context(nc.psum_tensor("zacc", [P, CB], f32))
        tacc = ctx.enter_context(nc.psum_tensor("tacc", [P, CB], f32))

        index_loaded = sem("index_loaded")
        index_copied = sem("index_copied")
        small_loaded = sem("small_loaded")
        dense_loaded = sem("dense_loaded")
        ident_made = sem("ident_made")
        band_made = sem("band_made")
        w_loaded = [sem(f"w_loaded{i}") for i in range(WRING)]
        rows_gathered = [sem(f"rows_gathered{i}") for i in range(GRING)]
        rows_transposed = sem("rows_transposed")
        emb_ready = sem("emb_ready")
        staged_ready = sem("staged_ready")
        u_ready = sem("u_ready")
        prod_ready = sem("prod_ready")
        sums_done = sem("sums_done")
        z_copied = sem("z_copied")
        top_ready = sem("top_ready")
        top_copied = sem("top_copied")
        out_stored = sem("out_stored")
        block = ctx.enter_context(nc.Block())

        def emb_base(c, chunks_ahead):
            if isinstance(c, int):
                return (c + chunks_ahead) % 2 * T
            return (c - 1) * T if chunks_ahead else (2 - c) * T

        def chunks(engine, body, prologue=None):
            body(0, top=False, prefetch=True)
            with engine.Fori(1, CHUNKS - 1) as c:
                body(c, top=True, prefetch=True)
            body(CHUNKS - 1, top=True, prefetch=False)

        @block.sync
        def _(sp):
            sp.dma_start(index[:, :], ids[:, :]).then_inc(index_loaded, 16)
            sp.dma_start(w1s[:, :, :], w1).then_inc(small_loaded, 16)
            sp.dma_start(w2s[:, :, :], w2).then_inc(small_loaded, 16)
            sp.dma_start(w3s[:, :], w3).then_inc(small_loaded, 16)
            sp.dma_start(b1s[:, :], b1).then_inc(small_loaded, 16)
            sp.dma_start(b2s[:, :], b2).then_inc(small_loaded, 16)

            def body(c, top, prefetch):
                for s in range(WSLOTS):
                    if not (isinstance(c, int) and c * WSLOTS + s < WRING):
                        sp.wait_ge(u_ready, c * N + (s - WRING + 1) * WS)
                    sp.dma_start(weights[:, s % WRING, :],
                                 w_pairs[:, s * WS * P:(s + 1) * WS * P]).then_inc(w_loaded[s % WRING], 16)

            chunks(sp, body)
            sp.wait_ge(top_copied, CHUNKS * TOP_GROUPS)
            sp.dma_start(y, ysb[:, :]).then_inc(out_stored, 16)
            sp.wait_ge(out_stored, 16)

        @block.gpsimd
        def _(pool):
            pool.memset(ident[:, :], 0.0).then_inc(ident_made, 1)
            pool.wait_ge(ident_made, 1)
            pool.affine_select(out=ident[:, :], in_=ident[:, :], compare_op=ALU.not_equal, fill=1.0, base=0,
                               pattern=[[-1, P]], channel_multiplier=1).then_inc(ident_made, 1)
            pool.wait_ge(index_loaded, 16)

            def gather_chunk(c):
                if not (isinstance(c, int) and c == 0):
                    for i in range(GRING):
                        pool.wait_ge(rows_gathered[i], c * (T // GRING * 2 * SUB * 16))
                pool.tensor_copy(index_now[:, :], index[:, bass.ds(c * SUB * FIELDS, SUB * FIELDS)]
                                 ).then_inc(index_copied, 1)
                pool.wait_ge(index_copied, c + 1)
                for t in range(T):
                    if isinstance(c, int) and c == 0:
                        if t >= GRING:
                            pool.wait_ge(rows_transposed, (t - GRING) // 2 + 1)
                    else:
                        pool.wait_ge(rows_transposed, c * TSTEPS + (t - GRING) // 2 + 1)
                    pool.nop(nofuse=True)
                    for s in range(SUB):
                        for e in (0, 1):
                            f = 2 * t + e
                            col = s * FIELDS + f
                            pool.indirect_dma_start(
                                out=gathered[:, t % GRING, s, e * DIM:(e + 1) * DIM], out_offset=None,
                                in_=tables[f],
                                in_offset=bass.IndirectOffsetOnAxis(
                                    ap=index_now[:, col:col + 1].bitcast(u32), axis=0),
                            ).then_inc(rows_gathered[t % GRING], 16)

            gather_chunk(0)
            with pool.Fori(1, CHUNKS) as c:
                gather_chunk(c)

        @block.scalar
        def _(act):
            act.wait_ge(small_loaded, 5 * 16)

            def copy_emb(c, ahead, i):
                act.wait_ge(rows_transposed, (c + ahead) * TSTEPS + i + 1)
                if not (isinstance(c, int) and c + ahead < 2):
                    act.wait_ge(prod_ready, (c + ahead - 1) * N)
                act.nop(nofuse=True)
                nc.scalar.activation(emb[:, bass.ds(emb_base(c, ahead) + 2 * i, 2), :],
                                     u[:, t_buffer(ahead, i), :, :], ACT.Copy).then_inc(emb_ready, 1)

            def t_buffer(ahead, i):
                return PRE_U[i] if not ahead else BODY_U[("transpose", i)]

            def stage(c, ahead, k):
                act.wait_ge(emb_ready, (c + ahead) * TSTEPS + k // 2 + 1)
                if k >= XRING:
                    act.wait_ge(u_ready, (c + ahead) * N + LAST_OF_K[k - XRING + 1] + 1)
                elif not (isinstance(c, int) and c + ahead == 0):
                    before = T - XRING + k
                    act.wait_ge(u_ready, (c + ahead - 1) * N + LAST_OF_K[min(before + 1, T - 1)] + 1)
                act.nop(nofuse=True)
                nc.scalar.activation(staged[:, k % XRING, :],
                                     emb[:, bass.ds(emb_base(c, ahead) + k, 1), :].rearrange("p o n -> p (o n)"),
                                     ACT.Copy).then_inc(staged_ready, 1)

            def copy_z(c, g):
                act.wait_ge(sums_done, c * BATCHES + min((g + 1) * ZSTEPS // 2, BATCHES))
                if g == 0 and not (isinstance(c, int) and c == 0):
                    act.wait_ge(top_ready, (c - 1) * TOP_GROUPS + M1)
                rows = DENSE_ROW if g == ZG - 1 else P
                nc.scalar.activation(z[0:rows, g, :], zacc[0:rows, :], ACT.Copy).then_inc(z_copied, 1)
                if g == 0:
                    act.dma_start(z[DENSE_ROW:LASTK, ZG - 1, :],
                                  dense[:, bass.ds(c * CB, CB)]).then_inc(dense_loaded, 16)

            def copy_top(c, item):
                layer, m, _, _ = item
                done = {1: 0, 2: M1, 3: M1 + M2}[layer] + m
                act.wait_ge(top_ready, c * TOP_GROUPS + done + 1)
                if layer == 1:
                    ins = nc.scalar.activation(h1[:, m, :], tacc[:, :], ACT.Relu, bias=b1s[:, m:m + 1])
                elif layer == 2:
                    ins = nc.scalar.activation(h2[:, m, :], tacc[:, :], ACT.Relu, bias=b2s[:, m:m + 1])
                else:
                    act.nop(nofuse=True)
                    ins = nc.scalar.activation(ysb[0:1, bass.ds(c * CB, CB)], tacc[0:1, :], ACT.Copy)
                ins.then_inc(top_copied, 1)

            for i in range(TSTEPS):
                copy_emb(0, 0, i)
            stage(0, 0, 0)
            stage(0, 0, 1)

            def body(c, top, prefetch):
                for kind, x in chunk_order(top, prefetch):
                    if kind == "pairs":
                        for k in range(2, T):
                            if x == FIRST_OF_K[k - 1]:
                                stage(c, 0, k)
                    elif kind == "transpose":
                        copy_emb(c, 1, x)
                    elif kind == "sum":
                        if (x + 1) * 2 % ZSTEPS == 0:
                            copy_z(c, (x + 1) * 2 // ZSTEPS - 1)
                    elif x[3]:
                        copy_top(c - 1, x)
                if prefetch:
                    stage(c, 1, 0)
                    stage(c, 1, 1)
                copy_z(c, ZG - 1)

            chunks(act, body)
            for item in TOPS:
                if item[3]:
                    copy_top(CHUNKS - 1, item)

        @block.vector
        def _(dve):
            dve.memset(band[:, :], 0.0).then_inc(band_made, 1)
            dve.wait_ge(band_made, 1)
            dve.memset(band[0:DIM, 30:31], 1.0).then_inc(band_made, 1)
            dve.memset(band[DIM:P, 31:32], 1.0).then_inc(band_made, 1)

            def body(c, top, prefetch):
                for n, (kind, k, t) in enumerate(STEPS):
                    if n == 0:
                        dve.wait_ge(emb_ready, (c + 1) * TSTEPS)
                    dve.wait_ge(u_ready, c * N + n + 1)
                    if not (isinstance(c, int) and c * N + n < PRING):
                        dve.wait_ge(sums_done, c * BATCHES + (n - PRING) // 2 + 1)
                    if not isinstance(c, int):
                        dve.nop(nofuse=True)
                    b = BODY_U[("pairs", n)]
                    e0 = emb_base(c, 0)
                    if kind == "full":
                        x_t = emb[:, bass.ds(e0 + t, 1), :].broadcast_to([P, 2, CB])
                        nc.vector.tensor_tensor(prod[:, n % PRING, :, :], u[:, b, :, :], x_t,
                                                ALU.mult).then_inc(prod_ready, 1)
                    else:
                        nc.vector.tensor_tensor(prod[DIM:P, n % PRING, :, :], u[DIM:P, b, :, :],
                                                emb[DIM:P, bass.ds(e0 + k, 2), :],
                                                ALU.mult).then_inc(prod_ready, 1)

            chunks(dve, body)

        @block.tensor
        def _(pe):
            def transpose_step(c, ahead, i, b):
                for h in (0, 1):
                    t = 2 * i + h
                    turns = (c + ahead) * (T // GRING) + t // GRING + 1
                    pe.wait_ge(rows_gathered[t % GRING], turns * (2 * SUB * 16))
                    for s in range(SUB):
                        last = nc.tensor.transpose(u[:, b, h, s * P:(s + 1) * P],
                                                   gathered[:, t % GRING, s, :], ident[:, :])
                last.then_inc(rows_transposed, 1)

            def pair_step(c, n, b):
                kind, k, t = STEPS[n]
                if n % WS == 0:
                    s = n // WS
                    pe.wait_ge(w_loaded[s % WRING], (c * (WSLOTS // WRING) + s // WRING + 1) * 16)
                w0 = n % WS * P
                w = weights[:, n // WS % WRING, w0:w0 + P]
                if n == FIRST_OF_K[k + (kind == "half")] or n == 0:
                    pe.wait_ge(staged_ready, c * T + k + (kind == "half") + 1)
                if kind == "half":
                    pe.nop(nofuse=True)
                for h in (0, 1):
                    if kind == "full":
                        last = nc.tensor.matmul(u[:, b, h, :], w[h * DIM:(h + 1) * DIM, :],
                                                staged[h * DIM:(h + 1) * DIM, k % XRING, :], start=True, stop=True)
                    else:
                        last = nc.tensor.matmul(u[DIM:P, b, h, :], w[0:DIM, h * DIM:(h + 1) * DIM],
                                                staged[0:DIM, (k + h) % XRING, :], start=True, stop=True)
                last.then_inc(u_ready, 1)

            def sum_step(c, j):
                pe.wait_ge(prod_ready, c * N + 2 * j + 2)
                if j % (ZSTEPS // 2) == 0 and not (isinstance(c, int) and c == 0 and j == 0):
                    pe.wait_ge(z_copied, c * ZG + j // (ZSTEPS // 2))
                if STEPS[2 * j][0] == "half":
                    pe.nop(nofuse=True)
                for n in (2 * j, 2 * j + 1):
                    for h in (0, 1):
                        g, cg, q = z_place(n, h)
                        lo = 0 if STEPS[n][0] == "full" else DIM
                        ends = [s for s in range(2 * g * ZSTEPS, min(2 * (g + 1) * ZSTEPS, 2 * N))
                                if z_place(s // 2, s % 2)[1] == cg]
                        last = nc.tensor.matmul(zacc[32 * cg:32 * cg + 32, :], band[lo:P, 30 - 2 * q:62 - 2 * q],
                                                prod[lo:P, n % PRING, h, :], start=(q == 0),
                                                stop=(2 * n + h == ends[-1]))
                last.then_inc(sums_done, 1)

            def top_step(c, item):
                layer, m, q, end = item
                if q == 0:
                    group = {1: 0, 2: M1, 3: M1 + M2}[layer] + m
                    if not (isinstance(c, int) and c == 0 and group == 0):
                        pe.wait_ge(top_copied, c * TOP_GROUPS + group)
                if layer == 1 and m == 0:
                    pe.wait_ge(z_copied, c * ZG + q + 1)
                    if q == ZG - 1:
                        pe.wait_ge(dense_loaded, (c + 1) * 16)
                if layer == 1:
                    rows = LASTK if q == ZG - 1 else P
                    last = nc.tensor.matmul(tacc[:, :], w1s[0:rows, q, m * P:(m + 1) * P], z[0:rows, q, :],
                                            start=(q == 0), stop=end)
                elif layer == 2:
                    last = nc.tensor.matmul(tacc[:, :], w2s[:, q, m * P:(m + 1) * P], h1[:, q, :],
                                            start=(q == 0), stop=end)
                else:
                    last = nc.tensor.matmul(tacc[0:1, :], w3s[:, q:q + 1], h2[:, q, :], start=(q == 0), stop=end)
                if end:
                    last.then_inc(top_ready, 1)

            pe.wait_ge(ident_made, 2)
            pe.wait_ge(band_made, 3)
            pe.wait_ge(small_loaded, 5 * 16)
            for i in range(TSTEPS):
                if i >= UBUF:
                    pe.wait_ge(emb_ready, i - UBUF + 1)
                transpose_step(0, 0, i, PRE_U[i])

            def body(c, top, prefetch):
                order = chunk_order(top, prefetch)
                uses = [o for o in order if o[0] in ("pairs", "transpose")]
                for o in order:
                    if o in uses:
                        at = uses.index(o)
                        if at == 0:
                            pe.wait_ge(emb_ready, (c + 1) * TSTEPS)
                            if not (isinstance(c, int) and c == 0):
                                pe.wait_ge(prod_ready, c * N)
                        before = [p for p in uses[:at] if BODY_U[p] == BODY_U[o]]
                        if before:
                            kind, x = before[-1]
                            if kind == "pairs":
                                pe.wait_ge(prod_ready, c * N + x + 1)
                            else:
                                pe.wait_ge(emb_ready, (c + 1) * TSTEPS + x + 1)
                    if o[0] == "pairs":
                        pair_step(c, o[1], BODY_U[o])
                    elif o[0] == "transpose":
                        transpose_step(c, 1, o[1], BODY_U[o])
                    elif o[0] == "sum":
                        sum_step(c, o[1])
                    else:
                        top_step(c - 1, o[1])

            chunks(pe, body)
            for item in TOPS:
                top_step(CHUNKS - 1, item)


def _uses(prefetch):
    return [o for o in chunk_order(False, prefetch) if o[0] in ("pairs", "transpose")]


BODY_U = {o: i % UBUF for i, o in enumerate(_uses(True))}
PRE_U = [i % UBUF for i in range(TSTEPS)]


def kernel(**inputs):
    import numpy as np
    import concourse.bacc as bacc
    from concourse.bass_utils import run_bass_kernel_spmd

    nc = bacc.Bacc("TRN2", target_bir_lowering=False, num_devices=1)
    arrays = {}

    def given(name, a):
        a = np.ascontiguousarray(a)
        arrays[name] = a
        return nc.dram_tensor(name, a.shape, mybir.dt.from_np(a.dtype), kind="ExternalInput").ap()

    ids = np.asarray(inputs["ids"])
    ids = given("ids", ids.reshape(CHUNKS * SUB, P, FIELDS).transpose(1, 0, 2).reshape(P, -1))
    tables = [given(f"tbl_{f}", np.asarray(inputs[f"tbl_{f}"])) for f in range(FIELDS)]

    w = np.asarray(inputs["L0_rec_W"])

    def pair(i, j):
        return i * FIELDS - i * (i + 1) // 2 + (j - i - 1)

    w_pairs = np.zeros((P, N, P), w.dtype)
    for n, (kind, k, t) in enumerate(STEPS):
        for h in (0, 1):
            if kind == "full":
                for e in (0, 1):
                    w_pairs[h * DIM:(h + 1) * DIM, n, e * DIM:(e + 1) * DIM] = w[pair(2 * k + h, 2 * t + e)]
            else:
                w_pairs[0:DIM, n, h * DIM:(h + 1) * DIM] = w[pair(2 * (k + h), 2 * (k + h) + 1)]
    w_pairs = given("w_pairs", w_pairs.reshape(P, N * P))

    top1 = np.asarray(inputs["W_top1"])
    w1 = np.zeros((ZG * P, H1), top1.dtype)
    for row, p in z_rows():
        w1[row] = top1[p]
    w1[(ZG - 1) * P + DENSE_ROW:(ZG - 1) * P + LASTK] = top1[PAIRS:]
    w1 = given("w_top1", w1.reshape(ZG, P, H1).transpose(1, 0, 2))
    w2 = given("w_top2", np.asarray(inputs["W_top2"]).reshape(M1, P, H2).transpose(1, 0, 2))
    w3 = given("w_top3", np.asarray(inputs["W_top3"]).reshape(M2, P).T)
    b1 = given("b_top1", np.asarray(inputs["b_top1"]).reshape(M1, P).T)
    b2 = given("b_top2", np.asarray(inputs["b_top2"]).reshape(M2, P).T)
    dense = given("dense", np.asarray(inputs["dense_ctx"]).T)
    y = nc.dram_tensor("y", (BATCH, 1), mybir.dt.float32, kind="ExternalOutput").ap()
    pair_tower(nc, ids, tables, w_pairs, dense, w1, b1, w2, b2, w3, y.rearrange("b o -> o b"))
    r = run_bass_kernel_spmd(nc, [arrays], core_ids=[0])
    return r.results[0]["y"]
```

```python
import concourse.bass as bass
from concourse import mybir
from contextlib import ExitStack

BATCH, FIELDS, DIM = 2048, 40, 64
PAIRS = FIELDS * (FIELDS - 1) // 2
DENSE, H1, H2 = 16, 512, 256
VOCAB = [125000, 1000, 12500, 1000, 125000, 1250, 125000, 1250, 1000, 1000, 1000, 1000, 1000, 1000, 1000,
         1250, 1250, 12500, 1000, 1000, 1250, 1000, 1000, 1250, 12500, 12500, 12500, 1250, 1000, 1000,
         12500, 1250, 12500, 1250, 1250, 1250, 1250, 1250, 1250, 1250]
P = 128
CB = 512
CHUNKS = BATCH // CB
SUB = CB // P
T = FIELDS // 2


def step_list(blocks):
    steps, visits = [], []
    for lo, hi in blocks:
        for k in range(hi):
            first = len(steps)
            if k % 2 and k > lo:
                steps.append((len(visits), k - 1, None))
                visits[-1][2] = first
            steps += [(len(visits), k, t) for t in range(max(lo, k + 1), hi)]
            visits.append([k, first, len(steps) - 1])
    return steps, visits


N = T * T // 2
ZSTEPS = 32
ZG = -(-N // ZSTEPS)
DENSE_ROW = 96
LASTK = DENSE_ROW + DENSE
WS = 5
WSLOTS = N // WS
WRING = 4
RAWRING = 2
WCOLS = 2 * P
XRING = 4
GRING = 4
PRING = 4
UBUF = 3
TSTEPS = T // 2
LAG = 2
M1, M2 = H1 // P, H2 // P
TOP_GROUPS = M1 + M2 + 1
TOP_AT = 2
BATCHES = N // 2


def z_place(n, h):
    g = n // ZSTEPS
    s = 2 * (n - g * ZSTEPS) + h
    ways = 3 if g == ZG - 1 else 4
    return g, s % ways, s // ways


def pair(i, j):
    return i * FIELDS - i * (i + 1) // 2 + (j - i - 1)


TOPS = ([(1, m, q, q == ZG - 1) for m in range(M1) for q in range(ZG)] +
        [(2, m, q, q == M1 - 1) for m in range(M2) for q in range(M1)] +
        [(3, 0, q, q == M2 - 1) for q in range(M2)])


class Plan:

    def __init__(self, first, prefetch):
        self.first = first
        self.steps, self.visits = step_list([(0, 4), (4, 8), (8, 12), (12, T)] if first else [(0, T)])
        assert len(self.steps) == N and len(self.visits) % XRING == 0
        where = {s[1:]: n for n, s in enumerate(step_list([(0, T)])[0])}
        self.image = [where[s[1:]] for s in self.steps]
        out = []
        tops = [] if first else list(TOPS)
        own = 0
        staged = 0 if first else 2
        split = 0
        later = []
        ahead = [84 + 12 * i if first else 12 + 19 * i for i in range(TSTEPS)]

        def need(t):
            nonlocal own
            while first and own <= t // 2:
                out.append(("transpose", 0, own))
                own += 1

        for n, (v, k, t) in enumerate(self.steps):
            need(k + 1 if t is None else t)
            while later and later[0][0] <= n:
                out.append(later.pop(0)[1])
            while staged < len(self.visits) and self.visits[max(staged - 2, 0)][1] <= n and (
                    not first or self.visits[staged][0] // 2 < own):
                out.append(("stage", 0, staged))
                later.append((n if staged <= v + 1 else n + 2, ("spread", 0, staged)))
                staged += 1
            while later and later[0][0] <= n:
                out.append(later.pop(0)[1])
            while first and split < WSLOTS and (split - WRING + 1) * WS <= n:
                out.append(("split", split))
                split += 1
            if n >= TOP_AT and tops:
                out.append(("top", tops.pop(0)))
            out.append(("pairs", n))
            if prefetch and n in ahead:
                out.append(("transpose", 1, ahead.index(n)))
            if n % 2 and n >= LAG + 1:
                out.append(("sum", (n - 1 - LAG) // 2))
        assert staged == len(self.visits) and not later
        out += [("sum", j) for j in range((N - LAG) // 2, BATCHES)]
        if prefetch:
            out += [("stage", 1, 0), ("stage", 1, 1), ("spread", 1, 0), ("spread", 1, 1)]
        out.append(("last z",))
        self.order = out
        uses = [o for o in out if o[0] in ("pairs", "transpose")]
        self.buffer = {o: i % UBUF for i, o in enumerate(uses)}
        self.before = {o: uses[i - UBUF] if i >= UBUF else None for i, o in enumerate(uses)}

    def z_rows(self):
        out = []
        for n, (_, k, t) in enumerate(self.steps):
            for h in (0, 1):
                g, c, q = z_place(n, h)
                row = g * P + 32 * c + 2 * q
                if t is None:
                    out.append((row + 1, pair(2 * (k + h), 2 * (k + h) + 1)))
                else:
                    out += [(row + e, pair(2 * k + h, 2 * t + e)) for e in (0, 1)]
        return out


FIRST, MIDDLE, LAST = Plan(True, True), Plan(False, True), Plan(False, False)


def visits_before(c):
    if isinstance(c, int) and c == 0:
        return 0
    return len(FIRST.visits) + (c - 1) * T


def pair_tower(nc, ids, tables, w_pairs, dense, w1_first, w1_rest, b1, w2, b2, w3, y):
    f32, f32r = mybir.dt.float32, mybir.dt.float32r
    i32, u32 = mybir.dt.int32, mybir.dt.uint32
    ALU = mybir.AluOpType
    ACT = mybir.ActivationFunctionType

    ctx = ExitStack()
    with ctx:
        def sb(name, shape, dt=f32):
            return ctx.enter_context(nc.sbuf_tensor(name, shape, dt))

        def sem(name):
            return ctx.enter_context(nc.semaphore(name))

        w_split = nc.dram_tensor("w_split", (P, N * WCOLS), f32, kind="Internal").ap()
        weights = sb("weights", [P, WRING, WS * WCOLS], f32r)
        staged = sb("staged", [P, XRING, 2, 2, CB], f32r)
        index = sb("index", [P, CHUNKS * SUB * FIELDS], i32)
        index_now = sb("index_now", [P, SUB * FIELDS], i32)
        gathered = sb("gathered", [P, GRING, SUB, 2 * DIM])
        emb = sb("emb", [P, 2 * T, CB])
        prod = sb("prod", [P, PRING, 2, CB])
        z = sb("z", [P, ZG, CB])
        hidden = sb("hidden", [P, (M1 + M2) * CB])
        h1 = hidden[:, 0:M1 * CB].rearrange("p (m n) -> p m n", m=M1)
        h2 = hidden[:, M1 * CB:(M1 + M2) * CB].rearrange("p (m n) -> p m n", m=M2)
        raw = hidden[:, 0:RAWRING * WS * WCOLS].rearrange("p (r n) -> p r n", r=RAWRING)
        ysb = sb("ysb", [1, CB])
        w1s = sb("w1s", [P, ZG, H1])
        w2s = sb("w2s", [P, M1, H2])
        w3s = sb("w3s", [P, M2])
        b1s = sb("b1s", [P, M1])
        b2s = sb("b2s", [P, M2])
        ident = sb("ident", [P, P])
        band = sb("band", [P, 62])
        u = ctx.enter_context(nc.psum_tensor("u", [P, UBUF, 2, CB], f32))
        zacc = ctx.enter_context(nc.psum_tensor("zacc", [P, CB], f32))
        tacc = ctx.enter_context(nc.psum_tensor("tacc", [P, CB], f32))

        index_loaded = sem("index_loaded")
        index_copied = sem("index_copied")
        small_loaded = sem("small_loaded")
        w1_loaded = sem("w1_loaded")
        dense_loaded = sem("dense_loaded")
        ident_made = sem("ident_made")
        band_made = sem("band_made")
        raw_loaded = [sem(f"raw_loaded{i}") for i in range(RAWRING)]
        high_ready = sem("high_ready")
        split_ready = sem("split_ready")
        w_stored = [sem(f"w_stored{i}") for i in range(WRING)]
        w_loaded = [sem(f"w_loaded{i}") for i in range(WRING)]
        rows_gathered = [sem(f"rows_gathered{i}") for i in range(GRING)]
        rows_transposed = sem("rows_transposed")
        emb_ready = sem("emb_ready")
        x_high = sem("x_high")
        x_low = sem("x_low")
        staged_ready = sem("staged_ready")
        u_ready = sem("u_ready")
        prod_ready = sem("prod_ready")
        sums_done = sem("sums_done")
        z_copied = sem("z_copied")
        top_ready = sem("top_ready")
        top_copied = sem("top_copied")
        out_stored = sem("out_stored")
        block = ctx.enter_context(nc.Block())

        def emb_base(c, ahead):
            if isinstance(c, int):
                return (c + ahead) % 2 * T
            return (c - 1) * T if ahead else (2 - c) * T

        def alone(engine, c):
            if not isinstance(c, int):
                engine.nop(nofuse=True)

        def chunks(engine, body):
            body(0, FIRST)
            with engine.Fori(1, CHUNKS - 1) as c:
                body(c, MIDDLE)
            body(CHUNKS - 1, LAST)

        @block.sync
        def _(sp):
            sp.dma_start(index[:, :], ids[:, :]).then_inc(index_loaded, 16)

            def load_raw(s):
                if s >= RAWRING:
                    sp.wait_ge(split_ready, s - RAWRING + 1)
                for r in range(WS):
                    at = FIRST.image[s * WS + r] * WCOLS
                    for half in (0, 1):
                        sp.dma_start(raw[half * DIM:(half + 1) * DIM, s % RAWRING, r * WCOLS:(r + 1) * WCOLS],
                                     w_pairs[:, at:at + WCOLS]).then_inc(raw_loaded[s % RAWRING], 16)

            for s in range(RAWRING):
                load_raw(s)
            sp.dma_start(w2s[:, :, :], w2).then_inc(small_loaded, 16)
            sp.dma_start(w3s[:, :], w3).then_inc(small_loaded, 16)
            sp.dma_start(b1s[:, :], b1).then_inc(small_loaded, 16)
            sp.dma_start(b2s[:, :], b2).then_inc(small_loaded, 16)
            sp.dma_start(w1s[:, :, :], w1_first).then_inc(w1_loaded, 16)
            for s in range(WSLOTS):
                sp.wait_ge(split_ready, s + 1)
                for r in range(WS):
                    at = FIRST.image[s * WS + r] * WCOLS
                    sp.dma_start(w_split[:, at:at + WCOLS], weights[:, s % WRING, r * WCOLS:(r + 1) * WCOLS].bitcast(f32)
                                 ).then_inc(w_stored[s % WRING], 16)
                if s + RAWRING < WSLOTS:
                    load_raw(s + RAWRING)
            for i in range(WRING):
                sp.wait_ge(w_stored[i], WSLOTS // WRING * WS * 16)

            def load(c):
                for s in range(WSLOTS):
                    sp.wait_ge(u_ready, c * N + (s - WRING + 1) * WS)
                    sp.dma_start(weights[:, s % WRING, :].bitcast(f32),
                                 w_split[:, s * WS * WCOLS:(s + 1) * WS * WCOLS]).then_inc(w_loaded[s % WRING], 16)

            with sp.Fori(1, CHUNKS) as c:
                load(c)

        @block.gpsimd
        def _(pool):
            pool.memset(ident[:, :], 0.0).then_inc(ident_made, 1)
            pool.wait_ge(ident_made, 1)
            pool.affine_select(out=ident[:, :], in_=ident[:, :], compare_op=ALU.not_equal, fill=1.0, base=0,
                               pattern=[[-1, P]], channel_multiplier=1).then_inc(ident_made, 1)
            pool.wait_ge(index_loaded, 16)

            def gather_chunk(c):
                if not (isinstance(c, int) and c == 0):
                    for i in range(GRING):
                        pool.wait_ge(rows_gathered[i], c * (T // GRING * 2 * SUB * 16))
                pool.tensor_copy(index_now[:, :], index[:, bass.ds(c * SUB * FIELDS, SUB * FIELDS)]
                                 ).then_inc(index_copied, 1)
                pool.wait_ge(index_copied, c + 1)
                for t in range(T):
                    if not (isinstance(c, int) and c == 0 and t < GRING):
                        pool.wait_ge(rows_transposed, c * TSTEPS + (t - GRING) // 2 + 1)
                    alone(pool, c)
                    for s in range(SUB):
                        for e in (0, 1):
                            f = 2 * t + e
                            col = s * FIELDS + f
                            pool.indirect_dma_start(
                                out=gathered[:, t % GRING, s, e * DIM:(e + 1) * DIM], out_offset=None,
                                in_=tables[f],
                                in_offset=bass.IndirectOffsetOnAxis(
                                    ap=index_now[:, col:col + 1].bitcast(u32), axis=0),
                            ).then_inc(rows_gathered[t % GRING], 16)

            gather_chunk(0)
            with pool.Fori(1, CHUNKS) as c:
                gather_chunk(c)

        def slot_is_new(c, v):
            return isinstance(c, int) and c == 0 and v < XRING

        def staged_slot_free(engine, c, v, plan):
            if v >= XRING:
                engine.wait_ge(u_ready, c * N + plan.visits[v - XRING][2] + 1)
            elif not slot_is_new(c, v):
                engine.wait_ge(u_ready, (c - 1) * N + last_use(v) + 1)

        def last_use(v):
            return max(p.visits[len(p.visits) - XRING + v][2] for p in (FIRST, MIDDLE))

        @block.scalar
        def _(act):
            def copy_emb(c, ahead, i, plan):
                act.wait_ge(rows_transposed, (c + ahead) * TSTEPS + i + 1)
                if not (isinstance(c, int) and c + ahead < 2):
                    act.wait_ge(prod_ready, (c + ahead - 1) * N)
                alone(act, c)
                nc.scalar.activation(emb[:, bass.ds(emb_base(c, ahead) + 2 * i, 2), :],
                                     u[:, plan.buffer["transpose", ahead, i], :, :], ACT.Copy).then_inc(emb_ready, 1)

            def stage(c, ahead, v, plan):
                k = MIDDLE.visits[v][0] if ahead else plan.visits[v][0]
                act.wait_ge(emb_ready, (c + ahead) * TSTEPS + k // 2 + 1)
                staged_slot_free(act, c + ahead, v, plan)
                alone(act, c)
                for e in (0, 1):
                    x = emb[e * DIM:(e + 1) * DIM, bass.ds(emb_base(c, ahead) + k, 1), :].rearrange("p o n -> p (o n)")
                    for half in (0, 1):
                        ins = nc.scalar.activation(staged[half * DIM:(half + 1) * DIM, v % XRING, e, 0, :], x,
                                                   ACT.Copy)
                ins.then_inc(x_high, 1)

            def spread(c, ahead, v):
                act.wait_ge(x_low, visits_before(c + ahead) + v + 1)
                for e in (0, 1):
                    low = staged[:, v % XRING, e, 1, :]
                    ins = nc.scalar.activation(low[(1 - e) * DIM:(2 - e) * DIM, :],
                                               low[e * DIM:(e + 1) * DIM, :].bitcast(f32), ACT.Copy)
                ins.then_inc(staged_ready, 1)

            def split_high(s):
                act.wait_ge(raw_loaded[s % RAWRING], (s // RAWRING + 1) * 2 * WS * 16)
                if s >= WRING:
                    act.wait_ge(u_ready, (s - WRING + 1) * WS)
                    act.wait_ge(w_stored[s % WRING], s // WRING * WS * 16)
                nc.scalar.activation(weights[:, s % WRING, :], raw[:, s % RAWRING, :], ACT.Copy
                                     ).then_inc(high_ready, 1)

            def copy_z(c, g):
                act.wait_ge(sums_done, c * BATCHES + min((g + 1) * ZSTEPS // 2, BATCHES))
                if g == 0 and not (isinstance(c, int) and c == 0):
                    act.wait_ge(top_ready, (c - 1) * TOP_GROUPS + M1)
                rows = DENSE_ROW if g == ZG - 1 else P
                nc.scalar.activation(z[0:rows, g, :], zacc[0:rows, :], ACT.Copy).then_inc(z_copied, 1)
                if g == 0:
                    act.dma_start(z[DENSE_ROW:LASTK, ZG - 1, :],
                                  dense[:, bass.ds(c * CB, CB)]).then_inc(dense_loaded, 16)

            def copy_top(c, item):
                layer, m, _, _ = item
                done = {1: 0, 2: M1, 3: M1 + M2}[layer] + m
                act.wait_ge(top_ready, c * TOP_GROUPS + done + 1)
                if layer == 1:
                    ins = nc.scalar.activation(h1[:, m, :], tacc[:, :], ACT.Relu, bias=b1s[:, m:m + 1])
                elif layer == 2:
                    ins = nc.scalar.activation(h2[:, m, :], tacc[:, :], ACT.Relu, bias=b2s[:, m:m + 1])
                else:
                    ins = nc.scalar.activation(ysb[0:1, :], tacc[0:1, :], ACT.Copy)
                ins.then_inc(top_copied, 1)
                if layer == 3:
                    act.wait_ge(top_copied, (c + 1) * TOP_GROUPS)
                    act.dma_start(y[:, bass.ds(c * CB, CB)], ysb[0:1, :]).then_inc(out_stored, 16)
                    act.wait_ge(out_stored, (c + 1) * 16)

            def body(c, plan):
                for o in plan.order:
                    if o[0] == "transpose":
                        copy_emb(c, o[1], o[2], plan)
                    elif o[0] == "stage":
                        stage(c, o[1], o[2], plan)
                    elif o[0] == "spread":
                        spread(c, o[1], o[2])
                    elif o[0] == "split":
                        split_high(o[1])
                    elif o[0] == "sum" and (o[1] + 1) * 2 % ZSTEPS == 0:
                        copy_z(c, (o[1] + 1) * 2 // ZSTEPS - 1)
                    elif o[0] == "last z":
                        copy_z(c, ZG - 1)
                    elif o[0] == "top" and o[1][3]:
                        copy_top(c - 1, o[1])
                        if o[1][0] == 1 and o[1][1] == M1 - 1 and plan is MIDDLE:
                            act.dma_start(w1s[:, :, :], w1_rest).then_inc(w1_loaded, 16)

            act.wait_ge(small_loaded, 4 * 16)
            chunks(act, body)
            for item in TOPS:
                if item[3]:
                    copy_top(CHUNKS - 1, item)

        @block.vector
        def _(dve):
            dve.memset(band[:, :], 0.0).then_inc(band_made, 1)
            dve.wait_ge(band_made, 1)
            dve.memset(band[0:DIM, 30:31], 1.0).then_inc(band_made, 1)
            dve.memset(band[DIM:P, 31:32], 1.0).then_inc(band_made, 1)

            def low_parts(c, ahead, v, plan):
                k = MIDDLE.visits[v][0] if ahead else plan.visits[v][0]
                dve.wait_ge(x_high, visits_before(c + ahead) + v + 1)
                alone(dve, c)
                for e in (0, 1):
                    own = slice(e * DIM, (e + 1) * DIM)
                    x = emb[own, bass.ds(emb_base(c, ahead) + k, 1), :].rearrange("p o n -> p (o n)")
                    ins = nc.vector.tensor_tensor(staged[own, v % XRING, e, 1, :], x,
                                                  staged[own, v % XRING, e, 0, :].bitcast(f32), ALU.subtract)
                ins.then_inc(x_low, 1)

            def split_low(s):
                dve.wait_ge(high_ready, s + 1)
                w = weights[DIM:P, s % WRING, :]
                nc.vector.tensor_tensor(w, raw[DIM:P, s % RAWRING, :], w.bitcast(f32), ALU.subtract
                                        ).then_inc(split_ready, 1)

            def multiply(c, n, plan):
                _, k, t = plan.steps[n]
                if plan is FIRST:
                    dve.wait_ge(emb_ready, (k + 1 if t is None else t) // 2 + 1)
                elif n == 0:
                    dve.wait_ge(emb_ready, (c + 1) * TSTEPS)
                dve.wait_ge(u_ready, c * N + n + 1)
                if not (isinstance(c, int) and c * N + n < PRING):
                    dve.wait_ge(sums_done, c * BATCHES + (n - PRING) // 2 + 1)
                alone(dve, c)
                if t is None:
                    x = emb[:, bass.ds(emb_base(c, 0) + k, 2), :]
                else:
                    x = emb[:, bass.ds(emb_base(c, 0) + t, 1), :].broadcast_to([P, 2, CB])
                nc.vector.tensor_tensor(prod[:, n % PRING, :, :], u[:, plan.buffer["pairs", n], :, :], x,
                                        ALU.mult).then_inc(prod_ready, 1)

            def body(c, plan):
                for o in plan.order:
                    if o[0] == "stage":
                        low_parts(c, o[1], o[2], plan)
                    elif o[0] == "split":
                        split_low(o[1])
                    elif o[0] == "pairs":
                        multiply(c, o[1], plan)

            chunks(dve, body)

        @block.tensor
        def _(pe):
            def transpose_step(c, ahead, i, b):
                for h in (0, 1):
                    t = 2 * i + h
                    turns = (c + ahead) * (T // GRING) + t // GRING + 1
                    pe.wait_ge(rows_gathered[t % GRING], turns * (2 * SUB * 16))
                    for s in range(SUB):
                        last = nc.tensor.transpose(u[:, b, h, s * P:(s + 1) * P],
                                                   gathered[:, t % GRING, s, :], ident[:, :])
                last.then_inc(rows_transposed, 1)

            def pair_step(c, n, plan):
                v, k, t = plan.steps[n]
                s = n // WS
                if n % WS == 0:
                    if plan is FIRST:
                        pe.wait_ge(split_ready, s + 1)
                    else:
                        pe.wait_ge(w_loaded[s % WRING], ((c - 1) * (WSLOTS // WRING) + s // WRING + 1) * 16)
                if n == plan.visits[v][1] or n == 0:
                    pe.wait_ge(staged_ready, visits_before(c) + v + 1)
                for h in (0, 1):
                    w0 = (n % WS * 2 + h) * P
                    w = weights[:, s % WRING, w0:w0 + P]
                    x = staged[:, (v if t is not None else v - 1 + h) % XRING, h if t is not None else 0, :, :]
                    for part in (0, 1):
                        last = nc.tensor.matmul(u[:, plan.buffer["pairs", n], h, :], w, x[:, part, :],
                                                start=(part == 0), stop=(part == 1))
                last.then_inc(u_ready, 1)

            def sum_step(c, j):
                pe.wait_ge(prod_ready, c * N + 2 * j + 2)
                if j % (ZSTEPS // 2) == 0 and not (isinstance(c, int) and c == 0 and j == 0):
                    pe.wait_ge(z_copied, c * ZG + j // (ZSTEPS // 2))
                for n in (2 * j, 2 * j + 1):
                    for h in (0, 1):
                        g, cg, q = z_place(n, h)
                        end = not any(z_place(s // 2, s % 2)[:2] == (g, cg) for s in range(2 * n + h + 1, 2 * N))
                        last = nc.tensor.matmul(zacc[32 * cg:32 * cg + 32, :], band[:, 30 - 2 * q:62 - 2 * q],
                                                prod[:, n % PRING, h, :], start=(q == 0), stop=end)
                last.then_inc(sums_done, 1)

            def top_step(c, item):
                layer, m, q, end = item
                if q == 0:
                    group = {1: 0, 2: M1, 3: M1 + M2}[layer] + m
                    if not (isinstance(c, int) and c == 0 and group == 0):
                        if isinstance(c, int) or group:
                            pe.wait_ge(top_copied, c * TOP_GROUPS + group)
                if layer == 1 and m == 0:
                    pe.wait_ge(z_copied, c * ZG + q + 1)
                    if q == 0:
                        pe.wait_ge(w1_loaded, (min(c, 2) + 1) * 16 if isinstance(c, int) else (c + 1) * 16)
                    if q == ZG - 1:
                        pe.wait_ge(dense_loaded, (c + 1) * 16)
                if layer == 1:
                    rows = LASTK if q == ZG - 1 else P
                    last = nc.tensor.matmul(tacc[:, :], w1s[0:rows, q, m * P:(m + 1) * P], z[0:rows, q, :],
                                            start=(q == 0), stop=end)
                elif layer == 2:
                    last = nc.tensor.matmul(tacc[:, :], w2s[:, q, m * P:(m + 1) * P], h1[:, q, :],
                                            start=(q == 0), stop=end)
                else:
                    last = nc.tensor.matmul(tacc[0:1, :], w3s[:, q:q + 1], h2[:, q, :], start=(q == 0), stop=end)
                if end:
                    last.then_inc(top_ready, 1)

            pe.wait_ge(ident_made, 2)
            pe.wait_ge(band_made, 3)
            pe.wait_ge(small_loaded, 4 * 16)

            def body(c, plan):
                begun = False
                for o in plan.order:
                    if o[0] in ("pairs", "transpose"):
                        if not begun and plan is not FIRST:
                            pe.wait_ge(emb_ready, (c + 1) * TSTEPS)
                            pe.wait_ge(prod_ready, c * N)
                        begun = True
                        if plan.before[o]:
                            if plan.before[o][0] == "pairs":
                                pe.wait_ge(prod_ready, c * N + plan.before[o][1] + 1)
                            else:
                                pe.wait_ge(emb_ready, (c + plan.before[o][1]) * TSTEPS + plan.before[o][2] + 1)
                    if o[0] == "pairs":
                        pair_step(c, o[1], plan)
                    elif o[0] == "transpose":
                        transpose_step(c, o[1], o[2], plan.buffer[o])
                    elif o[0] == "sum":
                        sum_step(c, o[1])
                    elif o[0] == "top":
                        top_step(c - 1, o[1])

            chunks(pe, body)
            for item in TOPS:
                top_step(CHUNKS - 1, item)


def kernel(**inputs):
    import numpy as np
    import concourse.bacc as bacc
    from concourse.bass_utils import run_bass_kernel_spmd

    nc = bacc.Bacc("TRN2", target_bir_lowering=False, num_devices=1)
    arrays = {}

    def given(name, a):
        a = np.ascontiguousarray(a)
        arrays[name] = a
        return nc.dram_tensor(name, a.shape, mybir.dt.from_np(a.dtype), kind="ExternalInput").ap()

    ids = np.asarray(inputs["ids"])
    ids = given("ids", ids.reshape(CHUNKS * SUB, P, FIELDS).transpose(1, 0, 2).reshape(P, -1))
    tables = [given(f"tbl_{f}", np.asarray(inputs[f"tbl_{f}"])) for f in range(FIELDS)]

    w = np.asarray(inputs["L0_rec_W"])

    w_pairs = np.zeros((DIM, N, 2, P), w.dtype)
    for n, (_, k, t) in enumerate(MIDDLE.steps):
        for h in (0, 1):
            if t is None:
                w_pairs[:, n, h, DIM:] = w[pair(2 * (k + h), 2 * (k + h) + 1)]
            else:
                for e in (0, 1):
                    w_pairs[:, n, h, e * DIM:(e + 1) * DIM] = w[pair(2 * k + h, 2 * t + e)]
    w_pairs = given("w_pairs", w_pairs.reshape(DIM, N * WCOLS))

    top1 = np.asarray(inputs["W_top1"])
    w1 = []
    for name, plan in (("w_top1_first", FIRST), ("w_top1_rest", MIDDLE)):
        rows = np.zeros((ZG * P, H1), top1.dtype)
        for row, p in plan.z_rows():
            rows[row] = top1[p]
        rows[(ZG - 1) * P + DENSE_ROW:(ZG - 1) * P + LASTK] = top1[PAIRS:]
        w1.append(given(name, rows.reshape(ZG, P, H1).transpose(1, 0, 2)))
    w2 = given("w_top2", np.asarray(inputs["W_top2"]).reshape(M1, P, H2).transpose(1, 0, 2))
    w3 = given("w_top3", np.asarray(inputs["W_top3"]).reshape(M2, P).T)
    b1 = given("b_top1", np.asarray(inputs["b_top1"]).reshape(M1, P).T)
    b2 = given("b_top2", np.asarray(inputs["b_top2"]).reshape(M2, P).T)
    dense = given("dense", np.asarray(inputs["dense_ctx"]).T)
    y = nc.dram_tensor("y", (BATCH, 1), mybir.dt.float32, kind="ExternalOutput").ap()
    pair_tower(nc, ids, tables, w_pairs, dense, w1[0], w1[1], b1, w2, b2, w3, y.rearrange("b o -> o b"))
    r = run_bass_kernel_spmd(nc, [arrays], core_ids=[0])
    return r.results[0]["y"]
```

```python
import concourse.bass as bass
from concourse import mybir
from contextlib import ExitStack

BATCH, FIELDS, DIM = 2048, 40, 64
PAIRS = FIELDS * (FIELDS - 1) // 2
DENSE, H1, H2 = 16, 512, 256
VOCAB = [125000, 1000, 12500, 1000, 125000, 1250, 125000, 1250, 1000, 1000, 1000, 1000, 1000, 1000, 1000,
         1250, 1250, 12500, 1000, 1000, 1250, 1000, 1000, 1250, 12500, 12500, 12500, 1250, 1000, 1000,
         12500, 1250, 12500, 1250, 1250, 1250, 1250, 1250, 1250, 1250]
P = 128
CB = 512
CHUNKS = BATCH // CB
SUB = CB // P
T = FIELDS // 2


ROW_F = 8
ROW_I = P // ROW_F
ROW_T = T - ROW_F // 2


def step_list(blocks, rows):
    steps, visits = [], []
    for lo, hi in blocks:
        ks = [2 * i + h for j in range(T // 4) for i in (j, T // 2 - 1 - j) for h in (0, 1)] if hi == T else range(hi)
        for k in ks:
            first, v = len(steps), len(visits)
            if k % 2 and k > lo:
                steps.append(("half", v, k - 1, None))
                visits[-1][2] = first
            by_row = rows and 2 * k + 1 < ROW_I
            full = [("full", v, k, t) for t in range(max(lo, k + 1), ROW_T if by_row else hi)]
            if by_row:
                apart = (len(full) - 2) // 4
                for h in (0, 1):
                    if len(steps) % 2:
                        steps.append(full.pop(0))
                    for a in (0, 1):
                        steps += [("row", v, k, (h, a))] + full[:apart]
                        full = full[apart:]
            steps += full
            visits.append([k, first, len(steps) - 1])
    return steps, visits


N = T * T // 2
ZSTEPS = 32
Z_ORDER = [0, 1, 2, 3, 6, 4, 5]
ZG = len(Z_ORDER)
ZTWO = 2
DENSE_BLOCK, DENSE_ROW = 5, 96
LASTK = DENSE_ROW + DENSE
WS = 5
WSLOTS = N // WS
WRING = 4
RAWRING = 3
WCOLS = 2 * P
HALF = WS * WCOLS // 2
SPLIT_BEFORE, SPLIT_AHEAD = [4, 8, 12, 15, 17], 7
XRING = 4
GRING = 4
PRING = 4
UBUF = 3
TSTEPS = T // 2
SPLIT_LAG = 2
STAGE_LAG = 2
LAG = 2
M1, M2 = H1 // P, H2 // P
TOP_GROUPS = M1 + M2 + 1
W12_AT = [10, 17, 22, 26]
TOP_AT = list(range(2, 80, 5)) + list(range(80, 146, 3))


def pair(i, j):
    return i * FIELDS - i * (i + 1) // 2 + (j - i - 1)


TOPS = ([(1, m, q, q == Z_ORDER[-1]) for m in range(M1) for q in Z_ORDER] +
        [(2, m, q, q == M1 - 1) for m in range(M2) for q in range(M1)] +
        [(3, 0, q, q == M2 - 1) for q in range(M2)])


class Plan:

    def __init__(self, first, prefetch):
        self.first = first
        self.steps, self.visits = (step_list([(0, 4), (4, 8), (8, 12), (12, T)], False) if first else
                                   step_list([(0, T)], True))
        self.columns = [n for n, s in enumerate(self.steps) if s[0] != "row"]
        self.rows = [n for n, s in enumerate(self.steps) if s[0] == "row"]
        self.batches = len(self.columns) // 2
        self.groups = -(-len(self.columns) // ZSTEPS)
        self.places = []
        pair_at = None
        for n, s in enumerate(self.steps):
            if s[0] == "row" and s[3][1] == 0:
                pair_at = [n, n + 1]
                self.places.append(pair_at)
            elif s[0] == "row":
                self.places.append(pair_at)
                pair_at = None
            else:
                self.places.append([n + 1] if pair_at else [n])
        self.free_after = [max(n for n in range(N) if set(self.places[n]) & set(range(x * WS, x * WS + WS)))
                           for x in range(WSLOTS)]
        assert self.groups == (ZG if first else ZG - 1) and len(self.columns) % PRING == 0
        assert len(self.steps) == N and len(self.visits) % XRING == 0
        out = []
        tops = [] if first else list(TOPS)
        own = 0
        staged = 0 if first else 2
        split = loaded = 0
        later = []
        half_split = []
        own_at = {21: 4, 30: 5, 43: 6, 53: 7, 63: 8, 72: 9}
        ahead = [82 + 12 * i if first else 24 + 17 * i for i in range(TSTEPS)]
        queue = [(t, e) for t in range(GRING) for e in (0, 1)] if prefetch else []
        summed = 0

        def take_later(n):
            while later and later[0][0] <= n:
                out.append(later.pop(0)[1])

        def need(t):
            nonlocal own, split, loaded
            while first and own <= t // 2:
                while half_split:
                    out.append(half_split.pop(0)[1])
                while own < len(SPLIT_BEFORE) and split < SPLIT_BEFORE[own]:
                    out.extend([("split", split), ("split low", split)])
                    split += 1
                    if loaded < WRING:
                        out.append(("load", loaded))
                        loaded += 1
                out.append(("transpose", 0, own))
                own += 1

        for n, (kind, v, k, t) in enumerate(self.steps):
            need(k + 1 if kind == "half" else t)
            if n in own_at:
                need(2 * own_at[n])
            take_later(n)
            more = True
            while staged <= v or more and staged < len(self.visits) and (
                    staged < XRING or self.visits[staged - XRING][2] < n) and (
                    not first or self.visits[staged][0] // 2 < own):
                more = False
                out.append(("stage", 0, staged))
                room = self.visits[staged][1] - n
                low = n + (min(STAGE_LAG, room // 3) if first else 0)
                later.append((low, ("low", 0, staged)))
                later.append((low + (min(2, room // 3) if first else min(8, room // 2)), ("spread", 0, staged)))
                staged += 1
            while later and any(o[2] <= v for _, o in later):
                out.append(later.pop(0)[1])
            assert staged > v
            take_later(n)
            while first and split < WSLOTS and (split - SPLIT_AHEAD) * WS <= n:
                out.append(("split", split))
                half_split.append((n + SPLIT_LAG, ("split low", split)))
                split += 1
            while half_split and half_split[0][0] <= n:
                out.append(half_split.pop(0)[1])
            while first and loaded < WSLOTS and (loaded - WRING + 1) * WS <= n:
                assert ("split low", loaded) in out
                out.append(("load", loaded))
                loaded += 1
            if n in TOP_AT and tops:
                out.append(("top", tops.pop(0)))
            out.append(("pairs", n))
            if prefetch and n in ahead:
                i = ahead.index(n)
                while queue and queue[0][0] <= 2 * i + 1:
                    out.append(("gather",) + queue.pop(0))
                out.append(("transpose", 1, i))
                queue += [(t, e) for t in (2 * i + GRING, 2 * i + GRING + 1) if t < T for e in (0, 1)]
            if queue and (not first and n % 4 == 0 or first and own == TSTEPS and (n % 3 == 0 or queue[0][0] < GRING)):
                out.append(("gather",) + queue.pop(0))
            if kind == "row":
                out.append(("reduce", n))
            if summed < self.batches and self.columns[2 * summed + 1] + LAG <= n:
                self.add_sum(out, summed)
                summed += 1
        assert staged == len(self.visits) and not later and not queue and not tops
        for j in range(summed, self.batches):
            self.add_sum(out, j)
        if prefetch:
            out += [("stage", 1, 0), ("low", 1, 0), ("stage", 1, 1), ("low", 1, 1), ("spread", 1, 0), ("spread", 1, 1)]
        out.append(("last z",))
        self.order = out
        uses = [o for o in out if o[0] in ("pairs", "transpose", "turn")]
        self.buffer = {o: i % UBUF for i, o in enumerate(uses)}
        self.before = {o: uses[i - UBUF] if i >= UBUF else None for i, o in enumerate(uses)}

    def add_sum(self, out, j):
        out.append(("sum", j))
        if self.rows and j + 1 == Z_ORDER.index(6) * ZSTEPS // 2:
            assert [o for o in out if o[0] == "reduce"][-1][1] == self.rows[-1]
            out.append(("turn",))

    def block(self, g):
        order = [q for q in Z_ORDER if q != 6 or not self.rows]
        return order[g]

    def z_place(self, m, h):
        g = m // ZSTEPS
        s = 2 * (m - g * ZSTEPS) + h
        ways = 3 if g == self.groups - 1 else 4
        return g, s % ways, s // ways

    def z_rows(self):
        out = []
        for m, n in enumerate(self.columns):
            kind, _, k, t = self.steps[n]
            for h in (0, 1):
                g, c, q = self.z_place(m, h)
                row = self.block(g) * P + 32 * c + 2 * q
                if kind == "half":
                    out.append((row + 1, pair(2 * (k + h), 2 * (k + h) + 1)))
                else:
                    out += [(row + e, pair(2 * k + h, 2 * t + e)) for e in (0, 1)]
        for n in self.rows:
            _, _, k, h = self.steps[n]
            i = 2 * k + h[0]
            out += [(6 * P + ROW_F * i + f, pair(i, FIELDS - ROW_F + f)) for f in range(ROW_F)]
        return out


FIRST, MIDDLE, LAST = Plan(True, True), Plan(False, True), Plan(False, False)


def slot_pieces():
    where = {(s[0],) + s[2:]: MIDDLE.places[i][0] for i, s in enumerate(MIDDLE.steps)}
    pieces = []
    for n, (kind, _, k, t) in enumerate(FIRST.steps):
        if (kind, k, t) in where:
            pieces.append((where[kind, k, t] * WCOLS, WCOLS, n * WCOLS))
        else:
            pieces += [(where["row", k, (h, 0)] * WCOLS + (t - ROW_T) * P, P, n * WCOLS + h * P) for h in (0, 1)]
    slots = [[] for _ in range(WSLOTS)]
    for at, size, source in sorted(pieces):
        slot, at = slots[at // (WS * WCOLS)], at % (WS * WCOLS)
        if slot and slot[-1][0] + slot[-1][1] == at and slot[-1][2] + slot[-1][1] == source:
            slot[-1] = (slot[-1][0], slot[-1][1] + size, slot[-1][2])
        else:
            slot.append((at, size, source))
    return slots


SLOT_PIECES = slot_pieces()


def loads_until(c, s):
    if isinstance(c, int) and c == 0:
        return s // WRING + 1
    return (WSLOTS // WRING + (c - 1) * sum(len(SLOT_PIECES[x]) for x in range(s % WRING, WSLOTS, WRING)) +
            sum(len(SLOT_PIECES[x]) for x in range(s % WRING, s + 1, WRING)))


def sums_before(c):
    if isinstance(c, int) and c == 0:
        return 0
    return FIRST.batches + (c - 1) * MIDDLE.batches


def visits_before(c):
    if isinstance(c, int) and c == 0:
        return 0
    return len(FIRST.visits) + (c - 1) * T


def pair_tower(nc, ids, tables, w_pairs, dense, w1, b1, w2, b2, w3, y):
    f32, f32r = mybir.dt.float32, mybir.dt.float32r
    i32, u32 = mybir.dt.int32, mybir.dt.uint32
    ALU = mybir.AluOpType
    ACT = mybir.ActivationFunctionType

    ctx = ExitStack()
    with ctx:
        def sb(name, shape, dt=f32):
            return ctx.enter_context(nc.sbuf_tensor(name, shape, dt))

        def sem(name):
            return ctx.enter_context(nc.semaphore(name))

        w_split = nc.dram_tensor("w_split", (P, N * WCOLS), f32, kind="Internal").ap()
        weights = sb("weights", [P, WRING, WS * WCOLS], f32r)
        staged = sb("staged", [P, XRING, 2, 2, CB], f32r)
        index_now = sb("index_now", [P, SUB * FIELDS], i32)
        gathered = sb("gathered", [P, GRING, SUB, 2 * DIM])
        emb = sb("emb", [P, 2 * T, CB])
        last_fields = sb("last_fields", [P, SUB, ROW_F * DIM])
        prod = sb("prod", [P, PRING, 2, CB])
        row_prod = sb("row_prod", [P, 2, ROW_F * DIM])
        row_sums = sb("row_sums", [P, SUB, P])
        z = sb("z", [P, ZG + ZTWO, CB])
        top_space = sb("top_space", [P, (M1 + 1) * CB + 2 * ZG * P])
        h1 = top_space[:, 0:M1 * CB].rearrange("p (m n) -> p m n", m=M1)
        ysb = top_space[0:1, M1 * CB:(M1 + 1) * CB]
        w12s = top_space[:, (M1 + 1) * CB:].rearrange("p (b q n) -> p b q n", b=2, q=ZG)
        raw = top_space[:, 0:RAWRING * HALF].rearrange("p (r n) -> p r n", r=RAWRING)
        high = top_space[:, RAWRING * HALF:2 * RAWRING * HALF].rearrange("p (r n) -> p r n", r=RAWRING)
        h2 = z[:, 3:3 + M2, :]
        w3s = sb("w3s", [P, M2])
        b1s = sb("b1s", [P, M1])
        b2s = sb("b2s", [P, M2])
        ident = sb("ident", [P, P])
        band = sb("band", [P, 62])
        u = ctx.enter_context(nc.psum_tensor("u", [P, UBUF, 2, CB], f32))
        zacc = ctx.enter_context(nc.psum_tensor("zacc", [P, CB], f32))
        tacc = ctx.enter_context(nc.psum_tensor("tacc", [P, CB], f32))

        index_loaded = sem("index_loaded")
        small_loaded = sem("small_loaded")
        w12_loaded = [sem(f"w12_loaded{i}") for i in (0, 1)]
        dense_loaded = sem("dense_loaded")
        ident_made = sem("ident_made")
        band_made = sem("band_made")
        raw_loaded = [sem(f"raw_loaded{i}") for i in range(RAWRING)]
        high_ready = sem("high_ready")
        split_ready = sem("split_ready")
        w_stored = [sem(f"w_stored{i}") for i in range(RAWRING)]
        w_loaded = [sem(f"w_loaded{i}") for i in range(WRING)]
        rows_gathered = [sem(f"rows_gathered{i}") for i in range(GRING)]
        rows_transposed = sem("rows_transposed")
        emb_ready = sem("emb_ready")
        last_kept = sem("last_kept")
        rows_reduced = sem("rows_reduced")
        rows_turned = sem("rows_turned")
        x_high = sem("x_high")
        x_low_first = sem("x_low_first")
        x_low_rest = sem("x_low_rest")
        staged_ready = sem("staged_ready")
        u_ready = sem("u_ready")
        prod_ready = sem("prod_ready")
        sums_done = sem("sums_done")
        z_copied = sem("z_copied")
        top_ready = sem("top_ready")
        top_copied = sem("top_copied")
        out_stored = sem("out_stored")
        block = ctx.enter_context(nc.Block())

        def emb_base(c, ahead):
            if isinstance(c, int):
                return (c + ahead) % 2 * T
            return (c - 1) * T if ahead else (2 - c) * T

        def z_block(c, ago, q):
            if q >= ZTWO:
                return z[:, q, :]
            if isinstance(c, int):
                return z[:, q + ZG * ((c - ago) % 2), :]
            place = (c - 1) * ZG + q if ago else (2 - c) * ZG + q
            return z[:, bass.ds(place, 1), :].rearrange("p o n -> p (o n)")

        def top_group(item):
            layer, m, _, _ = item
            return {1: 0, 2: M1, 3: M1 + M2}[layer] + m

        def last_accumulator(item):
            return (tacc[:, :], u[:, 0, 0, :], u[:, 0, 1, :])[top_group(item) % 3]

        def alone(engine, c):
            if not isinstance(c, int):
                engine.nop(nofuse=True)

        def chunks(engine, body):
            body(0, FIRST)
            with engine.Fori(1, CHUNKS - 1) as c:
                body(c, MIDDLE)
            body(CHUNKS - 1, LAST)

        def low_parts(engine, c, ahead, v, plan):
            k = MIDDLE.visits[v][0] if ahead else plan.visits[v][0]
            engine.wait_ge(x_high, visits_before(c + ahead) + v + 1)
            alone(engine, c)
            for e in (0, 1):
                own = slice(e * DIM, (e + 1) * DIM)
                x = emb[own, bass.ds(emb_base(c, ahead) + k, 1), :].rearrange("p o n -> p (o n)")
                ins = engine.tensor_tensor(staged[own, v % XRING, e, 1, :], x,
                                           staged[own, v % XRING, e, 0, :].bitcast(f32), ALU.subtract)
            ins.then_inc(x_low_first if plan is FIRST and not ahead else x_low_rest, 1)

        def split_low(engine, s):
            engine.wait_ge(high_ready, s + 1)
            engine.tensor_tensor(raw[:, s % RAWRING, :], raw[:, s % RAWRING, :], high[:, s % RAWRING, :],
                                 ALU.subtract).then_inc(split_ready, 1)

        @block.sync
        def _(sp):
            def load_raw(s):
                if s >= RAWRING:
                    sp.wait_ge(w_stored[s % RAWRING], (s // RAWRING) * 32)
                sp.dma_start(raw[:, s % RAWRING, :], w_pairs[:, s * HALF:(s + 1) * HALF]
                             ).then_inc(raw_loaded[s % RAWRING], 16)

            for s in range(RAWRING):
                load_raw(s)
            sp.dma_start(w3s[:, :], w3).then_inc(small_loaded, 16)
            sp.dma_start(b1s[:, :], b1).then_inc(small_loaded, 16)
            sp.dma_start(b2s[:, :], b2).then_inc(small_loaded, 16)
            for o in FIRST.order:
                if o[0] == "split low":
                    s = o[1]
                    sp.wait_ge(split_ready, s + 1)
                    for part, rows in ((high, slice(0, DIM)), (raw, slice(DIM, P))):
                        sp.dma_start(w_split[rows, s * 2 * HALF:(s + 1) * 2 * HALF].rearrange("p (h n) -> h p n", h=2),
                                     part[:, s % RAWRING, :]).then_inc(w_stored[s % RAWRING], 16)
                    if 1 <= s < WSLOTS - RAWRING + 1:
                        load_raw(s - 1 + RAWRING)
                elif o[0] == "load":
                    s = o[1]
                    sp.wait_ge(w_stored[s % RAWRING], (s // RAWRING + 1) * 32)
                    if s >= WRING:
                        sp.wait_ge(u_ready, (s - WRING + 1) * WS)
                    sp.dma_start(weights[:, s % WRING, :].bitcast(f32),
                                 w_split[:, s * WS * WCOLS:(s + 1) * WS * WCOLS]).then_inc(w_loaded[s % WRING], 16)

            def load_w12(image, b):
                if b < M1:
                    sp.dma_start(w12s[:, b % 2, :, :],
                                 w1[:, bass.ds(image, 1), b, :, :].rearrange("p o q n -> p (o q) n")
                                 ).then_inc(w12_loaded[b % 2], 16)
                else:
                    sp.dma_start(w12s[:, b % 2, 0:M1, :], w2[:, b - M1, :, :]).then_inc(w12_loaded[b % 2], 16)

            def body(c, plan):
                if plan is FIRST:
                    return
                image = 1 if plan is LAST else c - 1
                for s in range(WSLOTS):
                    if s < WRING:
                        sp.wait_ge(u_ready, (c - 1) * N + MIDDLE.free_after[s - WRING] + 1)
                    else:
                        sp.wait_ge(u_ready, c * N + plan.free_after[s - WRING] + 1)
                    if s < 2:
                        load_w12(image, s)
                    for at, size, source in SLOT_PIECES[s]:
                        sp.dma_start(weights[:, s % WRING, at:at + size].bitcast(f32),
                                     w_split[:, source:source + size]).then_inc(w_loaded[s % WRING], 16)
                    if s in W12_AT:
                        b = 2 + W12_AT.index(s)
                        sp.wait_ge(top_ready, (c - 1) * TOP_GROUPS + b - 1)
                        load_w12(image, b)

            chunks(sp, body)
            for b in range(M1 + M2):
                sp.wait_ge(top_ready, (CHUNKS - 1) * TOP_GROUPS + b - 1 if b > 1 else
                           (CHUNKS - 2) * TOP_GROUPS + M1 + M2 + b - 1)
                load_w12(1, b)

        @block.gpsimd
        def _(pool):
            pool.memset(ident[:, :], 0.0).then_inc(ident_made, 1)
            pool.wait_ge(ident_made, 1)
            pool.affine_select(out=ident[:, :], in_=ident[:, :], compare_op=ALU.not_equal, fill=1.0, base=0,
                               pattern=[[-1, P]], channel_multiplier=1).then_inc(ident_made, 1)
            def load_index(c):
                if not (isinstance(c, int) and c == 0):
                    for i in range(GRING):
                        pool.wait_ge(rows_gathered[i], c * (T // GRING * 2 * SUB * 16))
                alone(pool, c)
                pool.dma_start(index_now[:, :], ids[:, bass.ds(c * SUB * FIELDS, SUB * FIELDS)]
                               ).then_inc(index_loaded, 16)
                pool.wait_ge(index_loaded, (c + 1) * 16)

            def gather(c, t, e):
                if not (isinstance(c, int) and c == 0 and t < GRING):
                    pool.wait_ge(rows_transposed, c * TSTEPS + (t - GRING) // 2 + 1)
                    if t < GRING and not (isinstance(c, int) and c == 1):
                        pool.wait_ge(last_kept, 2 * (c - 1))
                pool.nop(nofuse=True)
                for s in range(SUB):
                    col = s * FIELDS + 2 * t + e
                    pool.indirect_dma_start(
                        out=gathered[:, t % GRING, s, e * DIM:(e + 1) * DIM], out_offset=None,
                        in_=tables[2 * t + e],
                        in_offset=bass.IndirectOffsetOnAxis(ap=index_now[:, col:col + 1].bitcast(u32), axis=0),
                    ).then_inc(rows_gathered[t % GRING], 16)

            load_index(0)
            for t in range(T):
                for e in (0, 1):
                    gather(0, t, e)

            def gathers_landed(c, t, e):
                for tt, halves in ((t, e + 1), (t - 1, 2)):
                    if tt >= 0:
                        pool.wait_ge(rows_gathered[tt % GRING],
                                     (c * (T // GRING) + tt // GRING) * (2 * SUB * 16) + halves * SUB * 16)

            def body(c, plan):
                gathered_last = (c, T - 1, 1)
                for o in plan.order:
                    if o[0] == "gather":
                        if o[1:] == (0, 0):
                            load_index(c + 1)
                        gather(c + 1, o[1], o[2])
                        gathered_last = (c + 1, o[1], o[2])
                    elif o[0] == "low" and not (plan is FIRST and o[1] == 0):
                        if gathered_last:
                            gathers_landed(*gathered_last)
                        low_parts(pool, c, o[1], o[2], plan)
                        pool.wait_ge(x_low_rest, (c + o[1] - 1) * T + o[2] + 1)
                        gathered_last = None

            chunks(pool, body)

        def slot_is_new(c, v):
            return isinstance(c, int) and c == 0 and v < XRING

        def staged_slot_free(engine, c, v, plan):
            if v >= XRING:
                engine.wait_ge(u_ready, c * N + plan.visits[v - XRING][2] + 1)
            elif not slot_is_new(c, v):
                engine.wait_ge(u_ready, (c - 1) * N + last_use(v) + 1)

        def last_use(v):
            return max(p.visits[len(p.visits) - XRING + v][2] for p in (FIRST, MIDDLE))

        @block.scalar
        def _(act):
            def copy_emb(c, ahead, i, plan):
                act.wait_ge(rows_transposed, (c + ahead) * TSTEPS + i + 1)
                if not (isinstance(c, int) and c + ahead < 2):
                    act.wait_ge(prod_ready, (c + ahead - 1) * N)
                alone(act, c)
                nc.scalar.activation(emb[:, bass.ds(emb_base(c, ahead) + 2 * i, 2), :],
                                     u[:, plan.buffer["transpose", ahead, i], :, :], ACT.Copy).then_inc(emb_ready, 1)
                if ahead and 2 * i >= ROW_T:
                    if not (isinstance(c, int) and c == 0):
                        act.wait_ge(prod_ready, c * N + plan.rows[-1] + 1)
                    for h in (0, 1):
                        t = 2 * i + h
                        ins = nc.scalar.activation(last_fields[:, :, (t - ROW_T) * P:(t - ROW_T + 1) * P],
                                                   gathered[:, t % GRING, :, :], ACT.Copy)
                    ins.then_inc(last_kept, 1)

            def stage(c, ahead, v, plan):
                k = MIDDLE.visits[v][0] if ahead else plan.visits[v][0]
                act.wait_ge(emb_ready, (c + ahead) * TSTEPS + k // 2 + 1)
                staged_slot_free(act, c + ahead, v, plan)
                alone(act, c)
                for e in (0, 1):
                    x = emb[e * DIM:(e + 1) * DIM, bass.ds(emb_base(c, ahead) + k, 1), :].rearrange("p o n -> p (o n)")
                    for half in (0, 1):
                        ins = nc.scalar.activation(staged[half * DIM:(half + 1) * DIM, v % XRING, e, 0, :], x,
                                                   ACT.Copy)
                ins.then_inc(x_high, 1)

            def spread(c, ahead, v):
                if isinstance(c, int) and c + ahead == 0:
                    act.wait_ge(x_low_first, v + 1)
                else:
                    act.wait_ge(x_low_rest, (c + ahead - 1) * T + v + 1)
                for e in (0, 1):
                    low = staged[:, v % XRING, e, 1, :]
                    ins = nc.scalar.activation(low[(1 - e) * DIM:(2 - e) * DIM, :],
                                               low[e * DIM:(e + 1) * DIM, :].bitcast(f32), ACT.Copy)
                ins.then_inc(staged_ready, 1)

            def split_high(s):
                act.wait_ge(raw_loaded[s % RAWRING], (s // RAWRING + 1) * 16)
                nc.scalar.activation(high[:, s % RAWRING, :].bitcast(f32r), raw[:, s % RAWRING, :], ACT.Copy
                                     ).then_inc(high_ready, 1)

            def copy_z(c, g, plan):
                act.wait_ge(sums_done, sums_before(c) + min((g + 1) * ZSTEPS // 2, plan.batches))
                if not (isinstance(c, int) and c == 0):
                    if g == ZTWO:
                        act.wait_ge(top_ready, (c - 1) * TOP_GROUPS + M1)
                    elif g == ZTWO + 1:
                        act.wait_ge(top_ready, c * TOP_GROUPS)
                    alone(act, c)
                q = plan.block(g)
                rows = DENSE_ROW if q == DENSE_BLOCK else P
                nc.scalar.activation(z_block(c, 0, q)[0:rows, :], zacc[0:rows, :], ACT.Copy).then_inc(z_copied, 1)
                if g == ZTWO:
                    act.dma_start(z[DENSE_ROW:LASTK, DENSE_BLOCK, :],
                                  dense[:, bass.ds(c * CB, CB)]).then_inc(dense_loaded, 16)

            def copy_top(c, item, tacc):
                layer, m, _, _ = item
                act.wait_ge(top_ready, c * TOP_GROUPS + top_group(item) + 1)
                if layer == 1:
                    ins = nc.scalar.activation(h1[:, m, :], tacc[:, :], ACT.Relu, bias=b1s[:, m:m + 1])
                elif layer == 2:
                    ins = nc.scalar.activation(h2[:, m, :], tacc[:, :], ACT.Relu, bias=b2s[:, m:m + 1])
                else:
                    ins = nc.scalar.activation(ysb, tacc[0:1, :], ACT.Copy)
                ins.then_inc(top_copied, 1)
                if layer == 3:
                    act.wait_ge(top_copied, (c + 1) * TOP_GROUPS)
                    act.dma_start(y[:, bass.ds(c * CB, CB)], ysb).then_inc(out_stored, 16)
                    act.wait_ge(out_stored, (c + 1) * 16)

            def body(c, plan):
                for o in plan.order:
                    if o[0] == "transpose":
                        copy_emb(c, o[1], o[2], plan)
                    elif o[0] == "stage":
                        stage(c, o[1], o[2], plan)
                    elif o[0] == "spread":
                        spread(c, o[1], o[2])
                    elif o[0] == "split":
                        split_high(o[1])
                    elif o[0] == "sum" and (o[1] + 1) * 2 % ZSTEPS == 0:
                        copy_z(c, (o[1] + 1) * 2 // ZSTEPS - 1, plan)
                    elif o[0] == "turn":
                        act.wait_ge(rows_turned, c)
                        nc.scalar.activation(z[:, 6, :], u[:, plan.buffer[o], 0, :], ACT.Copy).then_inc(z_copied, 1)
                    elif o[0] == "last z":
                        copy_z(c, plan.groups - 1, plan)
                    elif o[0] == "top" and o[1][3]:
                        copy_top(c - 1, o[1], tacc)

            act.wait_ge(small_loaded, 3 * 16)
            chunks(act, body)
            for item in TOPS:
                if item[3]:
                    copy_top(CHUNKS - 1, item, last_accumulator(item))

        @block.vector
        def _(dve):
            dve.memset(band[:, :], 0.0).then_inc(band_made, 1)
            dve.wait_ge(band_made, 1)
            dve.memset(band[0:DIM, 30:31], 1.0).then_inc(band_made, 1)
            dve.memset(band[DIM:P, 31:32], 1.0).then_inc(band_made, 1)

            def multiply(c, n, plan):
                kind, _, k, t = plan.steps[n]
                if plan is FIRST:
                    dve.wait_ge(emb_ready, (k + 1 if kind == "half" else t) // 2 + 1)
                elif n == 0:
                    dve.wait_ge(emb_ready, (c + 1) * TSTEPS)
                    dve.wait_ge(last_kept, 2 * c)
                dve.wait_ge(u_ready, c * N + n + 1)
                products = u[:, plan.buffer["pairs", n], :, :]
                if kind == "row":
                    j = plan.rows.index(n)
                    if j:
                        dve.wait_ge(rows_reduced, (c - 1) * 2 * ROW_I + j)
                    a = t[1]
                    nc.vector.tensor_tensor(row_prod[:, :, :], products, last_fields[:, 2 * a:2 * a + 2, :],
                                            ALU.mult).then_inc(prod_ready, 1)
                    return
                m = plan.columns.index(n)
                if not (isinstance(c, int) and c == 0 and m < PRING):
                    dve.wait_ge(sums_done, sums_before(c) + (m - PRING) // 2 + 1)
                alone(dve, c)
                if kind == "half":
                    x = emb[:, bass.ds(emb_base(c, 0) + k, 2), :]
                else:
                    x = emb[:, bass.ds(emb_base(c, 0) + t, 1), :].broadcast_to([P, 2, CB])
                nc.vector.tensor_tensor(prod[:, m % PRING, :, :], products, x, ALU.mult).then_inc(prod_ready, 1)

            def reduce_rows(c, n, plan):
                dve.wait_ge(prod_ready, c * N + n + 1)
                _, _, k, (h, a) = plan.steps[n]
                q = ROW_F * (2 * k + h)
                nc.vector.tensor_reduce(row_sums[:, 2 * a:2 * a + 2, q:q + ROW_F],
                                        row_prod[:, :, :].rearrange("p s (f e) -> p s f e", f=ROW_F),
                                        axis=mybir.AxisListType.X, op=ALU.add).then_inc(rows_reduced, 1)

            def body(c, plan):
                for o in plan.order:
                    if o[0] == "low" and plan is FIRST and o[1] == 0:
                        low_parts(dve, c, o[1], o[2], plan)
                    elif o[0] == "split low":
                        split_low(dve, o[1])
                    elif o[0] == "pairs":
                        multiply(c, o[1], plan)
                    elif o[0] == "reduce":
                        reduce_rows(c, o[1], plan)

            chunks(dve, body)

        @block.tensor
        def _(pe):
            def transpose_step(c, ahead, i, b):
                for h in (0, 1):
                    t = 2 * i + h
                    turns = (c + ahead) * (T // GRING) + t // GRING + 1
                    pe.wait_ge(rows_gathered[t % GRING], turns * (2 * SUB * 16))
                    for s in range(SUB):
                        last = nc.tensor.transpose(u[:, b, h, s * P:(s + 1) * P],
                                                   gathered[:, t % GRING, s, :], ident[:, :])
                last.then_inc(rows_transposed, 1)

            def pair_step(c, n, plan):
                kind, v, k, t = plan.steps[n]
                place = plan.places[n][0]
                for s in sorted({x // WS for x in plan.places[n]}):
                    if n and s <= max(x // WS for y in plan.places[:n] for x in y):
                        continue
                    pe.wait_ge(w_loaded[s % WRING], loads_until(c, s) * 16)
                if n == plan.visits[v][1] or n == 0:
                    pe.wait_ge(staged_ready, visits_before(c) + v + 1)
                w0 = place % (WRING * WS) * WCOLS
                w = weights[:, :, :].rearrange("p r n -> p (r n)")[:, w0:w0 + len(plan.places[n]) * WCOLS]
                out = u[:, plan.buffer["pairs", n], :, :]
                if kind == "row":
                    h, a = t
                    x = staged[:, v % XRING, h, :, :]
                    for b in (0, 1):
                        for part in (0, 1):
                            last = nc.tensor.matmul(out[:, b, :], x[:, part, (2 * a + b) * P:(2 * a + b + 1) * P], w,
                                                    start=(part == 0), stop=(part == 1))
                else:
                    for h in (0, 1):
                        x = staged[:, v % XRING, h, :, :] if kind == "full" else staged[:, (v - 1 + h) % XRING, 0, :, :]
                        for part in (0, 1):
                            last = nc.tensor.matmul(out[:, h, :], w[:, h * P:(h + 1) * P], x[:, part, :],
                                                    start=(part == 0), stop=(part == 1))
                last.then_inc(u_ready, 1)

            def sum_step(c, j, plan):
                pe.wait_ge(prod_ready, c * N + plan.columns[2 * j + 1] + 1)
                if j % (ZSTEPS // 2) == 0 and not (isinstance(c, int) and c == 0 and j == 0):
                    g = j // (ZSTEPS // 2)
                    pe.wait_ge(z_copied, c * ZG + (Z_ORDER.index(plan.block(g - 1)) + 1 if g else 0))
                tiles = [plan.z_place(m, h)[:2] for m in range(len(plan.columns)) for h in (0, 1)]
                for m in (2 * j, 2 * j + 1):
                    for h in (0, 1):
                        g, cg, q = plan.z_place(m, h)
                        last = nc.tensor.matmul(zacc[32 * cg:32 * cg + 32, :], band[:, 30 - 2 * q:62 - 2 * q],
                                                prod[:, m % PRING, h, :], start=(q == 0),
                                                stop=(g, cg) not in tiles[2 * m + h + 1:])
                last.then_inc(sums_done, 1)

            def turn_rows(c, b):
                pe.wait_ge(rows_reduced, c * 2 * ROW_I)
                for s in range(SUB):
                    last = nc.tensor.transpose(u[:, b, 0, s * P:(s + 1) * P], row_sums[:, s, :], ident[:, :])
                last.then_inc(rows_turned, 1)

            def top_step(now, ago, item, tacc):
                c = now - ago
                layer, m, q, end = item
                if q == 0:
                    group = top_group(item)
                    if ago:
                        if isinstance(c, int) and c > 0 or group:
                            pe.wait_ge(top_copied, c * TOP_GROUPS + group)
                    elif group == 0:
                        pe.wait_ge(top_copied, c * TOP_GROUPS)
                        pe.wait_ge(prod_ready, CHUNKS * N)
                    elif layer == 1:
                        if group == 3:
                            pe.wait_ge(top_copied, c * TOP_GROUPS + 1)
                    elif m == 0:
                        pe.wait_ge(top_copied, c * TOP_GROUPS + group)
                if layer < 3 and q == 0:
                    b = m if layer == 1 else M1 + m
                    pe.wait_ge(w12_loaded[b % 2], ((M1 + M2) // 2 * c + b // 2 + 1) * 16)
                if layer == 1 and m == 0:
                    pe.wait_ge(z_copied, c * ZG + Z_ORDER.index(q) + 1)
                    if q == DENSE_BLOCK:
                        pe.wait_ge(dense_loaded, (c + 1) * 16)
                if layer == 1:
                    rows = LASTK if q == DENSE_BLOCK else P
                    last = nc.tensor.matmul(tacc[:, :], w12s[0:rows, m % 2, q, :], z_block(now, ago, q)[0:rows, :],
                                            start=(q == 0), stop=end)
                elif layer == 2:
                    last = nc.tensor.matmul(tacc[:, :], w12s[:, (M1 + m) % 2, q, :], h1[:, q, :],
                                            start=(q == 0), stop=end)
                else:
                    last = nc.tensor.matmul(tacc[0:1, :], w3s[:, q:q + 1], h2[:, q, :], start=(q == 0), stop=end)
                if end:
                    last.then_inc(top_ready, 1)

            pe.wait_ge(ident_made, 2)
            pe.wait_ge(band_made, 3)
            pe.wait_ge(small_loaded, 3 * 16)

            def body(c, plan):
                begun = False
                for o in plan.order:
                    if o[0] in ("pairs", "transpose", "turn"):
                        if not begun and plan is not FIRST:
                            pe.wait_ge(emb_ready, (c + 1) * TSTEPS)
                            pe.wait_ge(prod_ready, c * N)
                            pe.wait_ge(z_copied, c * ZG - 1)
                        begun = True
                        if plan.before[o]:
                            if plan.before[o][0] == "pairs":
                                pe.wait_ge(prod_ready, c * N + plan.before[o][1] + 1)
                            elif plan.before[o][0] == "turn":
                                pe.wait_ge(z_copied, c * ZG + Z_ORDER.index(6) + 1)
                            else:
                                pe.wait_ge(emb_ready, (c + plan.before[o][1]) * TSTEPS + plan.before[o][2] + 1)
                    if o[0] == "pairs":
                        pair_step(c, o[1], plan)
                    elif o[0] == "transpose":
                        transpose_step(c, o[1], o[2], plan.buffer[o])
                    elif o[0] == "sum":
                        sum_step(c, o[1], plan)
                    elif o[0] == "turn":
                        turn_rows(c, plan.buffer[o])
                    elif o[0] == "top":
                        top_step(c, 1, o[1], tacc)

            chunks(pe, body)
            for item in TOPS:
                top_step(CHUNKS - 1, 0, item, last_accumulator(item))


def kernel(**inputs):
    import numpy as np
    import concourse.bacc as bacc
    from concourse.bass_utils import run_bass_kernel_spmd

    nc = bacc.Bacc("TRN2", target_bir_lowering=False, num_devices=1)
    arrays = {}

    def given(name, a):
        a = np.ascontiguousarray(a)
        arrays[name] = a
        return nc.dram_tensor(name, a.shape, mybir.dt.from_np(a.dtype), kind="ExternalInput").ap()

    ids = np.asarray(inputs["ids"])
    ids = given("ids", ids.reshape(CHUNKS * SUB, P, FIELDS).transpose(1, 0, 2).reshape(P, -1))
    tables = [given(f"tbl_{f}", np.asarray(inputs[f"tbl_{f}"])) for f in range(FIELDS)]

    w = np.asarray(inputs["L0_rec_W"])

    w_pairs = np.zeros((DIM, N, 2, P), w.dtype)
    for n, (kind, _, k, t) in enumerate(FIRST.steps):
        for h in (0, 1):
            if kind == "half":
                w_pairs[:, n, h, DIM:] = w[pair(2 * (k + h), 2 * (k + h) + 1)]
            else:
                for e in (0, 1):
                    w_pairs[:, n, h, e * DIM:(e + 1) * DIM] = w[pair(2 * k + h, 2 * t + e)]
    w_pairs = given("w_pairs", w_pairs.reshape(DIM, WSLOTS, 2, HALF).transpose(2, 0, 1, 3).reshape(P, -1))

    top1 = np.asarray(inputs["W_top1"])
    w1 = np.zeros((2, ZG * P, H1), top1.dtype)
    for image, plan in enumerate((FIRST, MIDDLE)):
        for row, p in plan.z_rows():
            w1[image, row] = top1[p]
        w1[image, DENSE_BLOCK * P + DENSE_ROW:DENSE_BLOCK * P + LASTK] = top1[PAIRS:]
    w1 = given("w_top1", w1.reshape(2, ZG, P, M1, P).transpose(2, 0, 3, 1, 4))
    w2 = given("w_top2", np.asarray(inputs["W_top2"]).reshape(M1, P, M2, P).transpose(1, 2, 0, 3))
    w3 = given("w_top3", np.asarray(inputs["W_top3"]).reshape(M2, P).T)
    b1 = given("b_top1", np.asarray(inputs["b_top1"]).reshape(M1, P).T)
    b2 = given("b_top2", np.asarray(inputs["b_top2"]).reshape(M2, P).T)
    dense = given("dense", np.asarray(inputs["dense_ctx"]).T)
    y = nc.dram_tensor("y", (BATCH, 1), mybir.dt.float32, kind="ExternalOutput").ap()
    pair_tower(nc, ids, tables, w_pairs, dense, w1, b1, w2, b2, w3, y.rearrange("b o -> o b"))
    r = run_bass_kernel_spmd(nc, [arrays], core_ids=[0])
    return r.results[0]["y"]
```
